# Optimizing a Trainium2 kernel written in Bass

```python
import numpy as np
import jax
import jax.numpy as jnp

def _softmax(x, axis=-1):
    return jax.nn.softmax(x, axis=axis)

def _gelu(x):
    return jax.nn.gelu(x, approximate=True)

def _silu(x):
    return jax.nn.silu(x)

def _sigmoid(x):
    return jax.nn.sigmoid(x)

def _layernorm(x, axis=-1, eps=1e-05):
    m = jnp.mean(x, axis=axis, keepdims=True)
    v = jnp.var(x, axis=axis, keepdims=True)
    return (x - m) / jnp.sqrt(v + eps)

def _scatter_add(tgt, idx, src, axis=0):
    return tgt.at[idx].add(src)

def _segment_sum(src, seg, n):
    return jax.ops.segment_sum(src, seg, n)
kernel_name = 'mk_audio_tower_d1_tok_aud1d1024_r4_9935ac'

def setup_inputs(seed: int=0):
    np.random.seed(seed)
    _w = jnp.asarray

    def _rec_inputs():
        import jax
        import jax.numpy as jnp
        _rk = jax.random.key(seed)
        x = -0.000392918 + 0.999932 * jax.random.normal(jax.random.fold_in(_rk, 1), (64, 4000), jnp.float32)
        return x
    x = _rec_inputs()

    def _L0_tok_setup():
        import jax, jax.numpy as jnp
        import numpy as np
        FRAME_SIZE = 256
        HOP_LENGTH = 64
        HIDDEN_DIM = 256
        BATCH = 32
        SIGNAL_LEN = 131072
        key = jax.random.key(seed)
        k1, k2 = jax.random.split(key)
        audio = jax.random.normal(k1, (BATCH, SIGNAL_LEN), dtype=jnp.float32)
        W = jax.random.normal(k2, (FRAME_SIZE, HIDDEN_DIM), dtype=jnp.float32) * 0.02
        b = jnp.zeros((HIDDEN_DIM,), dtype=jnp.float32)
        return {'audio': audio, 'W': W, 'b': b}
    _L0_tok_all = _L0_tok_setup()
    _L0_tok_in = {k: v for k, v in _L0_tok_all.items() if k in ('W', 'b')}
    del _L0_tok_all

    def _L0_attn_setup():
        import jax, jax.numpy as jnp
        import numpy as np
        from math import sqrt
        EMBED = 256
        HEADS = 16
        key = jax.random.key(seed)
        k1, k2, k3, k4, k5 = jax.random.split(key, 5)
        x = jax.random.normal(k1, (2, 512, EMBED), dtype=jnp.float32)
        s = 1.0 / sqrt(EMBED)
        W_qkv = jax.random.normal(k2, (EMBED, 3 * EMBED), dtype=jnp.float32) * s
        b_qkv = jax.random.normal(k3, (3 * EMBED,), dtype=jnp.float32) * 0.01
        W_out = jax.random.normal(k4, (EMBED, EMBED), dtype=jnp.float32) * s
        b_out = jax.random.normal(k5, (EMBED,), dtype=jnp.float32) * 0.01
        return {'x': x, 'W_qkv': W_qkv, 'b_qkv': b_qkv, 'W_out': W_out, 'b_out': b_out}
    _L0_attn_all = _L0_attn_setup()
    _L0_attn_in = {k: v for k, v in _L0_attn_all.items() if k in ('W_qkv', 'b_qkv', 'W_out', 'b_out')}
    del _L0_attn_all

    def _L0_ffn_setup():
        import jax, jax.numpy as jnp
        import numpy as np
        EXPERT_NUM = 8
        CAPACITY = 100
        key = jax.random.key(seed)
        k1, k2, k3 = jax.random.split(key, 3)
        B, S, H, E = (8, 512, 256, EXPERT_NUM)
        x = jax.random.normal(k1, (B, S, H), dtype=jnp.float32)
        w_gate = jax.random.normal(k2, (H, E), dtype=jnp.float32) * 0.02
        w_expert = jax.random.normal(k3, (H, H), dtype=jnp.float32) * 0.02
        b_expert = jnp.zeros((H,), dtype=jnp.float32)
        return {'x': x, 'w_gate': w_gate, 'w_expert': w_expert, 'b_expert': b_expert}
    _L0_ffn_all = _L0_ffn_setup()
    _L0_ffn_in = {k: v for k, v in _L0_ffn_all.items() if k in ('w_gate', 'w_expert', 'b_expert')}
    del _L0_ffn_all
    return {'x': x, 'L0_tok_W': _L0_tok_in['W'], 'L0_tok_b': _L0_tok_in['b'], 'L0_attn_W_qkv': _L0_attn_in['W_qkv'], 'L0_attn_b_qkv': _L0_attn_in['b_qkv'], 'L0_attn_W_out': _L0_attn_in['W_out'], 'L0_attn_b_out': _L0_attn_in['b_out'], 'L0_ffn_w_gate': _L0_ffn_in['w_gate'], 'L0_ffn_w_expert': _L0_ffn_in['w_expert'], 'L0_ffn_b_expert': _L0_ffn_in['b_expert']}

def reference(x, L0_tok_W, L0_tok_b, L0_attn_W_qkv, L0_attn_b_qkv, L0_attn_W_out, L0_attn_b_out, L0_ffn_w_gate, L0_ffn_w_expert, L0_ffn_b_expert):
    import jax
    import jax.numpy as jnp

    def _L0_tok_ref(audio, W, b):
        import jax, jax.numpy as jnp
        import numpy as np
        FRAME_SIZE = 256
        HOP_LENGTH = 64
        HIDDEN_DIM = 256
        BATCH = 32
        SIGNAL_LEN = 131072
        signal_length = audio.shape[1]
        num_frames = (signal_length - FRAME_SIZE) // HOP_LENGTH + 1
        indices = jnp.arange(FRAME_SIZE)[None, :] + jnp.arange(num_frames)[:, None] * HOP_LENGTH
        frames = audio[:, indices]
        window = jnp.hanning(FRAME_SIZE).astype(audio.dtype)
        frames = frames * window[None, None, :]
        out = jnp.einsum('bnf,fh->bnh', frames, W) + b
        return out

    def _L0_attn_ref(x, W_qkv, b_qkv, W_out, b_out):
        import jax, jax.numpy as jnp
        import numpy as np
        from math import sqrt
        EMBED = 256
        HEADS = 16
        B, N, E = x.shape
        H = HEADS
        d = E // H
        qkv = x @ W_qkv + b_qkv
        q, k, v = jnp.split(qkv, 3, axis=2)
        q = q.reshape(B, N, H, d)
        k = k.reshape(B, N, H, d)
        v = v.reshape(B, N, H, d)
        energy = jnp.einsum('bqhe,bkhe->bqhk', q, k)
        attn = jax.nn.softmax(energy, axis=-1) / sqrt(E)
        out = jnp.einsum('bihv,bvhd->bihd', attn, v)
        out = out.reshape(B, N, E)
        return out @ W_out + b_out

    def _L0_ffn_ref(x, w_gate, w_expert, b_expert):
        import jax, jax.numpy as jnp
        import numpy as np
        EXPERT_NUM = 8
        CAPACITY = 100
        B, S, H = x.shape
        E, C = (EXPERT_NUM, CAPACITY)
        hs = x.reshape(-1, H)
        logits = hs @ w_gate
        probs = jax.nn.softmax(logits, axis=1)
        best = jnp.argmax(probs, axis=1)
        mask = jax.nn.one_hot(best, E, dtype=jnp.int32)
        gate = jnp.sum(probs * mask.astype(probs.dtype), axis=1)
        locations = jnp.cumsum(mask, axis=0) - 1
        mask = mask * (locations < C).astype(jnp.int32)
        loc_sum = jnp.sum(locations * mask, axis=1)
        new_gates = gate[:, None] * mask.astype(probs.dtype)
        loc_oh = jax.nn.one_hot(loc_sum, C, dtype=probs.dtype)
        combine = new_gates[:, :, None] * loc_oh[:, None, :]
        dispatch = (combine != 0).astype(hs.dtype)
        dispatched = jnp.einsum('tec,th->ech', dispatch, hs).reshape(E * C, H)
        expert_out = dispatched @ w_expert + b_expert
        combined = combine.reshape(-1, E * C) @ expert_out
        return combined.reshape(B, S, H)
    h = _L0_tok_ref(x, L0_tok_W, L0_tok_b)
    h = h + _L0_attn_ref(_layernorm(h, axis=-1), L0_attn_W_qkv, L0_attn_b_qkv, L0_attn_W_out, L0_attn_b_out)
    h = h + _L0_ffn_ref(_layernorm(h, axis=-1), L0_ffn_w_gate, L0_ffn_w_expert, L0_ffn_b_expert)
    return h

_drawn_inputs = setup_inputs


def setup_inputs(seed=0):
    import zlib

    import numpy as np

    out = dict(_drawn_inputs(seed))
    spreads = {'L0_tok_b': (0.0, 0.1), 'L0_ffn_b_expert': (0.0, 0.1)}
    factors = {'L0_attn_b_qkv': 7.913}
    for name, (base, spread) in spreads.items():
        noise = np.random.default_rng([zlib.crc32(name.encode()), seed]).standard_normal(out[name].shape)
        drawn = base * np.exp(spread * noise) if base else spread * noise
        out[name] = jnp.asarray(drawn.astype(out[name].dtype))
    for name, factor in factors.items():
        out[name] = (out[name] * factor).astype(out[name].dtype)
    return out
```

```python
from contextlib import ExitStack

import concourse.bass as bass
from concourse import mybir

F32 = mybir.dt.float32
BF16 = mybir.dt.bfloat16
ALU = mybir.AluOpType
ACT = mybir.ActivationFunctionType
AX = mybir.AxisListType

BATCH, SAMPLES = 64, 4000
FRAME, HOP, HID = 256, 64, 256
HEADS, HD = 16, 16
EXPERTS, CAPACITY = 8, 100
TOK = (SAMPLES - FRAME) // HOP + 1
BLOCKS = TOK + 2
PAIRS = BATCH // 2
HALF = 64
P = 128
KC = HID // P
HG = HEADS // KC
HP = HEADS // 2
EPS = 1e-5


class Pair:

    def __init__(self, i, c):
        self.static = isinstance(i, int)
        self.i, self.c = i, c
        self.n = 2 * i + c
        self.par = c % 2
        self.half = i + c // 2

    def exists(self):
        return not self.static or 0 <= self.n < PAIRS

    def __add__(self, k):
        return Pair(self.i, self.c + k)

    def __sub__(self, k):
        return Pair(self.i, self.c - k)


LOOP_FROM, LOOP_TO = 4, PAIRS - 6
FIRST_STEP, LAST_STEP = -6, PAIRS + 1


def steps(eng, step):
    for t in range(FIRST_STEP, LOOP_FROM):
        step(Pair(0, t))
    with eng.Fori(0, (LOOP_TO - LOOP_FROM) // 2) as i:
        step(Pair(i, LOOP_FROM))
        step(Pair(i, LOOP_FROM + 1))
    for t in range(LOOP_TO, LAST_STEP + 1):
        step(Pair(0, t))


def after(eng, sem, pair, each=1):
    if pair.exists():
        eng.wait_ge(sem, (pair.n + 1) * each)


def after_latest(eng, *events):
    for sem, pair, each in events:
        if pair.exists():
            after(eng, sem, pair, each)
            return


def after_dma(eng, sems, pair, count):
    if pair.exists():
        eng.wait_ge(sems[pair.par], (pair.half + 1) * 16 * count)


def audio_tower(nc, x, tok_w, tok_b, w_qkv, b_qkv, w_out, b_out, w_gate, w_expert, b_expert,
                window, ident_in, order_in, out):
    with ExitStack() as ctx:
        def sb(name, shape, dt=F32):
            return ctx.enter_context(nc.sbuf_tensor(name, shape, dt))

        def ps(name, shape, dt=F32):
            return ctx.enter_context(nc.psum_tensor(name, shape, dt))

        def sem(name):
            return ctx.enter_context(nc.semaphore(name))

        ident = sb("ident", [P, P])
        order_f = sb("order_f", [P, 2 * P + EXPERTS])
        order = sb("order", [P, 2 * P], BF16)
        rank = order_f[:, 2 * P:2 * P + EXPERTS]
        win = sb("win", [P, KC])
        wtok = sb("wtok", [P, KC, HID])
        wqkv = sb("wqkv", [P, KC, 3 * HID])
        wout = sb("wout", [P, KC, HID])
        wffn = sb("wffn", [P, KC, HID + EXPERTS])
        tokb = sb("tokb", [P, HID])
        expb = sb("expb", [P, HID])
        outb = sb("outb", [P, HID])
        qkvb = sb("qkvb", [P, 3 * KC])
        qkb, vb = qkvb[:, 0:2 * KC], qkvb[:, 2 * KC:3 * KC]
        vb_wide = sb("vb_wide", [P, KC, P])
        sums_of = sb("sums_of", [P, 2 * HD])
        eps = sb("eps", [P, 1])
        half_exp = sb("half_exp", [P, 1])
        blk = [sb(f"blk{j}", [P, P]) for j in range(2)]
        blkT = [sb(f"blkT{j}", [P, P + 4]) for j in range(2)]
        h = [sb(f"h{j}", [P, HID]) for j in range(2)]
        xn = [sb(f"xn{j}", [P, HID]) for j in range(2)]
        xnT = [sb(f"xnT{j}", [P, KC, P]) for j in range(2)]
        qk = [sb(f"qk{j}", [P, 2 * KC, P]) for j in range(2)]
        kdiag = [sb(f"kdiag{j}", [P, KC * 2, HG, TOK]) for j in range(2)]
        vdiag = [sb(f"vdiag{j}", [P, 2, HP, 2 * HD]) for j in range(2)]
        top = [sb(f"top{j}", [P, HEADS]) for j in range(2)]
        shifted = [sb(f"shifted{j}", [P, HEADS, TOK]) for j in range(2)]
        prob = [sb(f"prob{j}", [P, HEADS, HALF]) for j in range(2)]
        probT = [sb(f"probT{j}", [P, HP, P]) for j in range(2)]
        rsum = [sb(f"rsum{j}", [P, KC, P]) for j in range(2)]
        attT = [sb(f"attT{j}", [P, KC, P]) for j in range(2)]
        h2 = [sb(f"h2_{j}", [P, HID]) for j in range(2)]
        xn2 = [sb(f"xn2_{j}", [P, HID]) for j in range(2)]
        xn2T = [sb(f"xn2T{j}", [P, KC, P]) for j in range(2)]
        y = [sb(f"y{j}", [P, HID]) for j in range(2)]
        res = [sb(f"res{j}", [P, HID]) for j in range(2)]
        stat = [[sb(f"stat{l}_{j}", [P, 6]) for j in range(2)] for l in range(2)]
        mv = [[sb(f"mv{l}_{j}", [P, 2]) for j in range(2)] for l in range(2)]
        veps = [[sb(f"veps{l}_{j}", [P, 1]) for j in range(2)] for l in range(2)]
        rstd = [[sb(f"rstd{l}_{j}", [P, 1]) for j in range(2)] for l in range(2)]
        resid = sb("resid", [P, PAIRS * HID])
        gtop = [sb(f"gtop{j}", [P, 1]) for j in range(2)]
        glog = [sb(f"glog{j}", [P, EXPERTS]) for j in range(2)]
        gexp = [sb(f"gexp{j}", [P, EXPERTS]) for j in range(2)]
        gsum = [sb(f"gsum{j}", [P, 1]) for j in range(2)]
        gate = [sb(f"gate{j}", [P, 1]) for j in range(2)]
        ghit = [sb(f"ghit{j}", [P, EXPERTS]) for j in range(2)]
        gbest = [sb(f"gbest{j}", [P, 1]) for j in range(2)]
        mask = [sb(f"mask{j}", [P, EXPERTS], BF16) for j in range(2)]
        place = [sb(f"place{j}", [P, EXPERTS]) for j in range(2)]
        keep8 = [sb(f"keep8_{j}", [P, EXPERTS]) for j in range(2)]
        kept = [sb(f"kept{j}", [P, 1]) for j in range(2)]
        weight = [sb(f"weight{j}", [P, 1]) for j in range(2)]
        carry = sb("carry", [P, EXPERTS])

        ps_s = ps("ps_s", [P, KC, 512])
        ps_pT = ps("ps_pT", [P, HP, P])
        ps_qk = ps("ps_qk", [P, 2 * KC, P])
        ps_t = ps("ps_t", [P, 512])
        ps_p = ps("ps_p", [P, 512])
        ps_o = ps("ps_o", [P, 2, KC, P])

        s_weights = sem("s_weights")
        s_blocks = [sem(f"s_blocks{j}") for j in range(2)]
        s_kdiag = [sem(f"s_kdiag{j}") for j in range(2)]
        s_stored = [sem(f"s_stored{j}") for j in range(2)]
        s_zeroed = sem("s_zeroed")
        s_ready = sem("s_ready")
        s_vb_wide = sem("s_vb_wide")
        s_vb_mm = sem("s_vb_mm")
        s_outb = sem("s_outb")
        blkT_done = sem("blkT_done")
        tok_done = sem("tok_done")
        xnT_done = sem("xnT_done")
        qk_done = sem("qk_done")
        v_done = sem("v_done")
        score_done = sem("score_done")
        pT_done = sem("pT_done")
        pv_done = sem("pv_done")
        out_done = sem("out_done")
        xn2T_done = sem("xn2T_done")
        ffn_done = sem("ffn_done")
        count_done = sem("count_done")
        blkT_ready = sem("blkT_ready")
        xnT_ready = sem("xnT_ready")
        v_ready = sem("v_ready")
        prob_ready = sem("prob_ready")
        pT_ready = sem("pT_ready")
        xn2T_ready = sem("xn2T_ready")
        gsum_ready = sem("gsum_ready")
        h_ready = sem("h_ready")
        stat_ready = [sem(f"stat_ready{l}") for l in range(2)]
        mv_ready = [sem(f"mv_ready{l}") for l in range(2)]
        xn_ready = sem("xn_ready")
        qk_ready = sem("qk_ready")
        top_ready = sem("top_ready")
        shifted_ready = sem("shifted_ready")
        rsum_ready = sem("rsum_ready")
        att_ready = sem("att_ready")
        h2_ready = sem("h2_ready")
        xn2_ready = sem("xn2_ready")
        y_ready = sem("y_ready")
        gtop_ready = sem("gtop_ready")
        glog_ready = sem("glog_ready")
        ghit_ready = sem("ghit_ready")
        gbest_ready = sem("gbest_ready")
        mask_ready = sem("mask_ready")
        gate_ready = sem("gate_ready")
        place_ready = sem("place_ready")
        kept_ready = sem("kept_ready")
        weight_ready = sem("weight_ready")
        carry_ready = sem("carry_ready")
        res_ready = sem("res_ready")
        veps_ready = [sem(f"veps_ready{l}") for l in range(2)]
        rstd_ready = [sem(f"rstd_ready{l}") for l in range(2)]
        resid_ready = sem("resid_ready")

        block = ctx.enter_context(nc.Block())

        def row(v):
            return bass.AP(tensor=v.tensor, offset=v.offset, ap=[[0, P], [1, v.shape[0]]])

        n_weights = 0

        @block.sync
        def _(sp):
            nonlocal n_weights
            loads = [
                (ident[:], ident_in),
                (win[:], window),
                (wtok[:], tok_w.rearrange("(c p) n -> p c n", p=P)),
                (tokb[:], row(tok_b)),
                (wqkv[:], w_qkv.rearrange("(c p) n -> p c n", p=P)),
                (qkvb[:], b_qkv),
                (wout[:], w_out.rearrange("(c p) n -> p c n", p=P)),
                (outb[:], row(b_out)),
                (wffn[:, :, 0:HID], w_expert.rearrange("(c p) n -> p c n", p=P)),
                (wffn[:, :, HID:], w_gate.rearrange("(c p) n -> p c n", p=P)),
                (expb[:], row(b_expert)),
                (order_f[:], order_in),
            ]

            def load_blocks(u):
                after(sp, blkT_done, u - 2)
                for b in range(2):
                    src = x[0:1, 0:P]
                    src = bass.AP(tensor=src.tensor, offset=(2 * u.n + b) * SAMPLES, ap=[[HOP, BLOCKS], [1, P]])
                    sp.dma_start(blk[u.par][HALF * b:HALF * b + BLOCKS, :], src).then_inc(s_blocks[u.par], 16)

            def spread_k(u):
                after(sp, qk_ready, u)
                after(sp, score_done, u - 2, KC)
                for hh in range(HG):
                    rows = slice(HD * hh, HD * hh + HD)
                    src = qk[u.par][rows, KC:2 * KC, :].rearrange("p c (b n) -> p (c b) n", b=2)[:, :, 0:TOK]
                    sp.dma_start(kdiag[u.par][rows, :, hh, :], src).then_inc(s_kdiag[u.par], 16)

            def store(u):
                after(sp, res_ready, u)
                for b in range(2):
                    dst = bass.AP(tensor=out.tensor, offset=(2 * u.n + b) * TOK * HID, ap=[[HID, TOK], [1, HID]])
                    sp.dma_start(dst, res[u.par][HALF * b:HALF * b + TOK, :]).then_inc(s_stored[u.par], 16)

            sp.wait_ge(s_zeroed, 1)
            first = True

            def step(t):
                nonlocal first
                if (t - 2).exists():
                    store(t - 2)
                if (t + 2).exists():
                    if t.static and t.n == -2:
                        sp.wait_ge(s_zeroed, 2)
                    spread_k(t + 2)
                if (t + 6).exists():
                    load_blocks(t + 6)
                if first:
                    for dst, src in loads:
                        sp.dma_start(dst, src).then_inc(s_weights, 16)
                    first = False

            n_weights = 16 * len(loads)
            steps(sp, step)
            for j in range(2):
                sp.wait_ge(s_stored[j], PAIRS // 2 * 2 * 16)

        @block.gpsimd
        def _(pool):
            for t_ in blk:
                last = nc.gpsimd.memset(t_[:], 0.0)
            last.then_inc(s_zeroed, 1)
            for t_ in kdiag:
                last = nc.gpsimd.memset(t_[:], 0.0)
            last.then_inc(s_zeroed, 1)
            nc.gpsimd.memset(eps[:], EPS)
            nc.gpsimd.memset(half_exp[:], -0.5)
            for t_ in blkT + vdiag + prob + [carry, sums_of]:
                last = nc.gpsimd.memset(t_[:], 0.0)
            last.then_inc(s_zeroed, 1)
            pool.wait_ge(s_zeroed, 3)

            def inverse_deviation(l, u):
                after(pool, mv_ready[l], u)
                nc.gpsimd.tensor_tensor(veps[l][u.par][:], mv[l][u.par][:, 1:2], eps[:], ALU.add).then_inc(veps_ready[l], 1)
                after(pool, veps_ready[l], u)
                nc.gpsimd.tensor_tensor(rstd[l][u.par][:], veps[l][u.par][:], half_exp[:], ALU.pow).then_inc(rstd_ready[l], 1)

            def step(t):
                if (t - 1).exists():
                    inverse_deviation(1, t - 1)
                if (t + 3).exists():
                    u = t + 3
                    inverse_deviation(0, u)
                    if u.static and u.n == 0:
                        pool.wait_ge(s_outb, 1)
                    after(pool, h_ready, u)
                    nc.gpsimd.tensor_tensor(resid[:, bass.ds(u.n * HID, HID)], h[u.par][:], outb[:], ALU.add).then_inc(resid_ready, 1)

            steps(pool, step)

        @block.scalar
        def _(act):
            act.wait_ge(s_zeroed, 3)

            def transposed_xn2(u):
                after(act, xn2T_done, u)
                after(act, ffn_done, u - 2)
                nc.scalar.copy(xn2T[u.par][:], ps_t[:, 0:HID]).then_inc(xn2T_ready, 1)

            def exponentials(u):
                after(act, shifted_ready, u, KC)
                after(act, pT_done, u - 2, KC)
                nc.scalar.activation(prob[u.par][:, :, 0:TOK], shifted[u.par][:], ACT.Exp).then_inc(prob_ready, 1)

            def values(u):
                after(act, v_done, u)
                after(act, pv_done, u - 2)
                for r in range(2):
                    rows = slice(HALF * r, HALF * r + HALF)
                    nc.scalar.copy(vdiag[u.par][rows, :, :, HD * r:HD * r + HD],
                                   ps_t[rows, 0:HID].rearrange("k (b p d) -> k b p d", b=2, d=HD)).then_inc(v_ready, 1)

            def gate_sum(u):
                after(act, glog_ready, u)
                nc.scalar.activation(gexp[u.par][:], glog[u.par][:], ACT.Exp, accum_out=gsum[u.par][:]).then_inc(gsum_ready, 1)

            def transposed_blocks(u):
                after(act, blkT_done, u)
                after(act, tok_done, u - 2)
                nc.scalar.copy(blkT[u.par][:, 0:P], ps_t[:, 0:P]).then_inc(blkT_ready, 1)

            def transposed_probs(u):
                after(act, pv_done, u - 2)
                for g in range(KC):
                    if u.exists():
                        act.wait_ge(pT_done, u.n * KC + g + 1)
                    part = slice(g * HP // KC, (g + 1) * HP // KC)
                    nc.scalar.copy(probT[u.par][:, part, :], ps_pT[:, part, :]).then_inc(pT_ready, 1)

            def transposed_xn(u):
                after(act, xnT_done, u)
                after(act, v_done, u - 2)
                nc.scalar.copy(xnT[u.par][:], ps_t[:, 0:HID]).then_inc(xnT_ready, 1)

            def step(t):
                if (t + 2).exists():
                    transposed_xn(t + 2)
                if (t - 2).exists():
                    gate_sum(t - 2)
                if t.exists():
                    exponentials(t)
                if (t + 1).exists():
                    values(t + 1)
                if t.exists():
                    transposed_probs(t)
                if (t - 1).exists():
                    transposed_xn2(t - 1)
                if (t + 4).exists():
                    transposed_blocks(t + 4)

            steps(act, step)

        @block.vector
        def _(dve):
            dve.wait_ge(s_weights, n_weights)
            dve.wait_ge(s_zeroed, 3)
            for c in range(KC):
                nc.vector.tensor_scalar(wtok[:, c, :], wtok[:, c, :], win[:, c:c + 1], None, ALU.mult)
                nc.vector.tensor_scalar(vb_wide[:, c, :], vb[:, c:c + 1].to_broadcast([P, P]), 1.0 / HID ** 0.5, None, ALU.mult).then_inc(s_vb_wide, 1)
            nc.vector.tensor_copy(order[:], order_f[:, 0:2 * P])
            for r in range(2):
                last = nc.vector.memset(sums_of[HALF * r:HALF * r + TOK, HD * r:HD * r + HD], HID ** 0.5)
            last.then_inc(s_ready, 1)
            dve.wait_ge(s_vb_mm, 1)
            nc.vector.tensor_tensor(outb[:], ps_p[:, 0:HID], outb[:], ALU.add).then_inc(s_outb, 1)

            def aggregate(l, u):
                nc.vector.bn_aggr(mv[l][u.par][:], stat[l][u.par][:]).then_inc(mv_ready[l], 1)

            def residual(u):
                after(dve, out_done, u)
                after(dve, resid_ready, u)
                nc.vector.tensor_tensor(h2[u.par][:], ps_p[:, 0:HID], resid[:, bass.ds(u.n * HID, HID)], ALU.add).then_inc(h2_ready, 1)
                after(dve, h2_ready, u)
                nc.vector.bn_stats(stat[1][u.par][:], h2[u.par][:]).then_inc(stat_ready[1], 1)

            def normalize2(u):
                after(dve, rstd_ready[1], u)
                after(dve, xn2T_done, u - 2)
                nc.vector.tensor_scalar(xn2[u.par][:], h2[u.par][:], mv[1][u.par][:, 0:1], rstd[1][u.par][:], ALU.subtract, ALU.mult).then_inc(xn2_ready, 1)

            def queue_places(u):
                j = u.par
                after(dve, gsum_ready, u)
                nc.vector.reciprocal(gate[j][:], gsum[j][:]).then_inc(gate_ready, 1)
                after(dve, count_done, u)
                after(dve, carry_ready, u - 1)
                nc.vector.tensor_tensor(place[j][:], ps_qk[:, 0, 0:EXPERTS], carry[:], ALU.add).then_inc(place_ready, 1)
                nc.vector.tensor_tensor(carry[:], ps_qk[:, 0, EXPERTS:2 * EXPERTS], carry[:], ALU.add).then_inc(carry_ready, 1)
                after(dve, place_ready, u)
                nc.vector.scalar_tensor_tensor(keep8[j][:], place[j][:], float(CAPACITY), mask[j][:], ALU.is_le, ALU.mult,
                                               accum_out=kept[j][:]).then_inc(kept_ready, 1)
                after(dve, kept_ready, u)
                after(dve, gate_ready, u)
                nc.vector.tensor_tensor(weight[j][:], kept[j][:], gate[j][:], ALU.mult).then_inc(weight_ready, 1)

            def result(u):
                after(dve, weight_ready, u)
                after_dma(dve, s_stored, u - 2, 2)
                nc.vector.scalar_tensor_tensor(res[u.par][:], y[u.par][:], weight[u.par][:], h2[u.par][:], ALU.mult, ALU.add).then_inc(res_ready, 1)

            def maximum(u, g):
                dve.wait_ge(score_done, u.n * KC + g + 1)
                nc.vector.tensor_reduce(top[u.par][:, g * HG:(g + 1) * HG],
                                        ps_s[:, g, 0:HG * TOK].rearrange("q (h k) -> q h k", h=HG), AX.X, ALU.max).then_inc(top_ready, 1)

            def shift(u, g):
                dve.wait_ge(top_ready, u.n * KC + g + 1)
                part = slice(g * HG, (g + 1) * HG)
                nc.vector.tensor_tensor(shifted[u.par][:, part, :], ps_s[:, g, 0:HG * TOK].rearrange("q (h k) -> q h k", h=HG),
                                        top[u.par][:, part].unsqueeze(2).to_broadcast([P, HG, TOK]), ALU.subtract).then_inc(shifted_ready, 1)

            def queries_keys(u):
                after(dve, qk_done, u)
                after(dve, score_done, u - 2, KC)
                after_dma(dve, s_kdiag, u - 2, HG)
                nc.vector.tensor_tensor(qk[u.par][:], ps_qk[:], qkb.unsqueeze(2).to_broadcast([P, 2 * KC, P]), ALU.add).then_inc(qk_ready, 1)

            def expert(u):
                j = u.par
                after(dve, ffn_done, u)
                nc.vector.tensor_reduce(gtop[j][:], ps_p[:, HID:HID + EXPERTS], AX.X, ALU.max).then_inc(gtop_ready, 1)
                nc.vector.tensor_tensor(y[j][:], ps_p[:, 0:HID], expb[:], ALU.add).then_inc(y_ready, 1)
                after(dve, gtop_ready, u)
                nc.vector.tensor_scalar(glog[j][:], ps_p[:, HID:HID + EXPERTS], gtop[j][:], None, ALU.subtract).then_inc(glog_ready, 1)

            def best_expert(u):
                j = u.par
                after(dve, glog_ready, u)
                nc.vector.scalar_tensor_tensor(ghit[j][:], glog[j][:], 0.0, rank, ALU.is_ge, ALU.mult).then_inc(ghit_ready, 1)
                after(dve, ghit_ready, u)
                nc.vector.tensor_reduce(gbest[j][:], ghit[j][:], AX.X, ALU.max).then_inc(gbest_ready, 1)
                after(dve, gbest_ready, u)
                nc.vector.tensor_scalar(mask[j][:], rank, gbest[j][:], None, ALU.is_equal).then_inc(mask_ready, 1)



            def tokens(u):
                after(dve, tok_done, u)
                after(dve, resid_ready, u - 2)
                nc.vector.tensor_tensor(h[u.par][:], ps_p[:, 0:HID], tokb[:], ALU.add).then_inc(h_ready, 1)
                after(dve, h_ready, u)
                nc.vector.bn_stats(stat[0][u.par][:], h[u.par][:]).then_inc(stat_ready[0], 1)

            def normalize(u):
                after(dve, rstd_ready[0], u)
                after(dve, xnT_done, u - 2)
                nc.vector.tensor_scalar(xn[u.par][:], h[u.par][:], mv[0][u.par][:, 0:1], rstd[0][u.par][:], ALU.subtract, ALU.mult).then_inc(xn_ready, 1)

            def inverse_sums(u):
                after(dve, pv_done, u)
                nc.vector.reciprocal(rsum[u.par][:], ps_o[:, 1, :, :]).then_inc(rsum_ready, 1)

            def attention_out(u):
                after(dve, rsum_ready, u)
                after(dve, out_done, u - 2)
                nc.vector.tensor_tensor(attT[u.par][:], ps_o[:, 0, :, :], rsum[u.par][:], ALU.mult).then_inc(att_ready, 1)

            def step(t):
                if (t - 1).exists():
                    inverse_sums(t - 1)
                if (t + 2).exists():
                    normalize(t + 2)
                if (t - 1).exists():
                    attention_out(t - 1)
                if (t - 2).exists():
                    expert(t - 2)
                if t.exists():
                    maximum(t, 0)
                    after(dve, prob_ready, t - 2)
                    shift(t, 0)
                    maximum(t, 1)
                    shift(t, 1)
                if (t - 1).exists():
                    residual(t - 1)
                    after(dve, stat_ready[1], t - 1)
                if (t + 2).exists():
                    queries_keys(t + 2)
                if (t - 1).exists():
                    aggregate(1, t - 1)
                if (t - 2).exists():
                    best_expert(t - 2)
                if (t - 1).exists():
                    normalize2(t - 1)
                if (t + 3).exists():
                    tokens(t + 3)
                    after(dve, stat_ready[0], t + 3)
                if (t - 2).exists():
                    queue_places(t - 2)
                if (t + 3).exists():
                    aggregate(0, t + 3)
                if (t - 2).exists():
                    result(t - 2)

            steps(dve, step)

        @block.tensor
        def _(pe):
            pe.wait_ge(s_weights, n_weights)
            pe.wait_ge(s_vb_wide, KC)
            pe.wait_ge(s_ready, 1)
            for c in range(KC):
                last = nc.tensor.matmul(ps_p[:, 0:HID], vb_wide[:, c, :], wout[:, c, :], start=(c == 0), stop=(c == KC - 1))
            last.then_inc(s_vb_mm, 1)
            pe.wait_ge(s_outb, 1)

            def transpose_blocks(u):
                after_dma(pe, s_blocks, u, 2)
                after_latest(pe, (xn2T_ready, u - 5, 1), (v_ready, u - 3, 2), (xnT_ready, u - 2, 1), (blkT_ready, u - 1, 1))
                nc.tensor.transpose(ps_t[:, 0:P], blk[u.par][:], ident[:]).then_inc(blkT_done, 1)

            def tokens(u):
                after(pe, blkT_ready, u)
                after_latest(pe, (h2_ready, u - 4, 1), (h_ready, u - 1, 1))
                for c in range(KC):
                    last = nc.tensor.matmul(ps_p[:, 0:HID], blkT[u.par][:, 2 * c:2 * c + P], wtok[:, c, :], start=(c == 0), stop=(c == KC - 1))
                last.then_inc(tok_done, 1)

            def transpose_xn(u):
                after(pe, xn_ready, u)
                after_latest(pe, (blkT_ready, u + 1, 1), (xn2T_ready, u - 4, 1))
                for c in range(KC):
                    last = nc.tensor.transpose(ps_t[:, P * c:P * c + P], xn[u.par][:, P * c:P * c + P], ident[:])
                last.then_inc(xnT_done, 1)

            def queries_keys(u):
                after(pe, xnT_ready, u)
                after(pe, carry_ready, u - 5)
                for m in range(2 * KC):
                    for c in range(KC):
                        last = nc.tensor.matmul(ps_qk[:, m, :], wqkv[:, c, P * m:P * m + P], xnT[u.par][:, c, :], start=(c == 0), stop=(c == KC - 1))
                last.then_inc(qk_done, 1)

            def values(u):
                after_latest(pe, (xnT_ready, u + 1, 1), (xn2T_ready, u - 3, 1))
                for b in range(2):
                    for c in range(KC):
                        for r in range(2):
                            w = wqkv[:, c, 2 * HID:3 * HID].rearrange("f (p r d) -> f r p d", r=2, d=HD)[:, r]
                            last = nc.tensor.matmul(ps_t[HALF * r:HALF * r + HALF, P * b:P * b + P],
                                                    xnT[u.par][:, c, HALF * b:HALF * b + HALF], w,
                                                    start=(c == 0), stop=(c == KC - 1))
                last.then_inc(v_done, 1)

            def scores(u):
                after_dma(pe, s_kdiag, u, HG)
                after(pe, qk_ready, u)
                after(pe, shifted_ready, u - 1, KC)
                for g in range(KC):
                    for b in range(2):
                        last = nc.tensor.matmul(ps_s[HALF * b:HALF * b + HALF, g, 0:HG * TOK],
                                                qk[u.par][:, g, HALF * b:HALF * b + HALF],
                                                kdiag[u.par][:, 2 * g + b, :, :].rearrange("p h k -> p (h k)"), start=True, stop=True)
                    last.then_inc(score_done, 1)

            def transpose_probs(u):
                after(pe, prob_ready, u)
                after(pe, pT_ready, u - 1, KC)
                for p in range(HP):
                    last = nc.tensor.transpose(ps_pT[:, p, :], prob[u.par][:, 2 * p:2 * p + 2, :].rearrange("q h k -> q (h k)"), ident[:])
                    if p % (HP // KC) == HP // KC - 1:
                        last.then_inc(pT_done, 1)

            def weighted_values(u):
                after(pe, pT_ready, u, KC)
                after(pe, v_ready, u, 2)
                after(pe, att_ready, u - 1)
                quads = HP // KC
                for g in range(KC):
                    for b in range(2):
                        for c in range(quads):
                            p = g * quads + c
                            nc.tensor.matmul(ps_o[2 * HD * c:2 * HD * (c + 1), 0, g, HALF * b:HALF * b + HALF],
                                             vdiag[u.par][:, b, p, :], probT[u.par][:, p, HALF * b:HALF * b + HALF], start=True, stop=True)
                for c in range(quads):
                    last = nc.tensor.matmul(ps_o[2 * HD * c:2 * HD * (c + 1), 1, :, :], sums_of[:], probT[u.par][:, c::quads, :], start=True, stop=True)
                last.then_inc(pv_done, 1)

            def project(u):
                after(pe, att_ready, u)
                after(pe, y_ready, u - 1)
                after(pe, glog_ready, u - 1)
                for c in range(KC):
                    last = nc.tensor.matmul(ps_p[:, 0:HID], attT[u.par][:, c, :], wout[:, c, :], start=(c == 0), stop=(c == KC - 1))
                last.then_inc(out_done, 1)

            def transpose_xn2(u):
                after(pe, xn2_ready, u)
                after_latest(pe, (v_ready, u + 2, 2), (xn2T_ready, u - 1, 1))
                for c in range(KC):
                    last = nc.tensor.transpose(ps_t[:, P * c:P * c + P], xn2[u.par][:, P * c:P * c + P], ident[:])
                last.then_inc(xn2T_done, 1)

            def expert(u):
                after(pe, xn2T_ready, u)
                after_latest(pe, (h_ready, u + 4, 1), (h2_ready, u, 1))
                for c in range(KC):
                    last = nc.tensor.matmul(ps_p[:, 0:HID + EXPERTS], xn2T[u.par][:, c, :], wffn[:, c, :], start=(c == 0), stop=(c == KC - 1))
                last.then_inc(ffn_done, 1)

            def counts(u):
                after(pe, mask_ready, u)
                after_latest(pe, (qk_ready, u + 4, 1), (carry_ready, u - 1, 1))
                for c in range(2):
                    last = nc.tensor.matmul(ps_qk[:, 0, EXPERTS * c:EXPERTS * (c + 1)], order[:, P * c:P * c + P], mask[u.par][:], start=True, stop=True)
                last.then_inc(count_done, 1)

            def step(t):
                if t.exists():
                    scores(t)
                if (t + 2).exists():
                    transpose_xn(t + 2)
                if (t - 1).exists():
                    project(t - 1)
                if (t + 2).exists():
                    queries_keys(t + 2)
                if (t + 1).exists():
                    values(t + 1)
                if t.exists():
                    transpose_probs(t)
                if (t - 2).exists():
                    counts(t - 2)
                if (t - 1).exists():
                    transpose_xn2(t - 1)
                if (t + 3).exists():
                    tokens(t + 3)
                if (t + 4).exists():
                    transpose_blocks(t + 4)
                if t.exists():
                    weighted_values(t)
                if (t - 1).exists():
                    expert(t - 1)

            steps(pe, step)


_INS = ["x", "L0_tok_W", "L0_tok_b", "L0_attn_W_qkv", "L0_attn_b_qkv", "L0_attn_W_out", "L0_attn_b_out",
        "L0_ffn_w_gate", "L0_ffn_w_expert", "L0_ffn_b_expert"]


def kernel(**inputs):
    import numpy as np
    import concourse.bacc as bacc
    from concourse.bass_utils import run_bass_kernel_spmd

    window = np.hanning(FRAME).astype(np.float32).reshape(KC, P).T
    ident = np.eye(P, dtype=np.float32)
    real = (np.arange(P) % HALF < TOK)[:, None]
    upto = np.arange(P)[:, None] <= np.arange(P)[None, :]
    rank = np.broadcast_to(EXPERTS - np.arange(EXPERTS), (P, EXPERTS))
    order = np.concatenate([upto & real, np.broadcast_to(real, (P, P)), rank], 1).astype(np.float32)

    inputs = dict(inputs, L0_attn_b_qkv=np.asarray(inputs["L0_attn_b_qkv"]).reshape(3 * KC, P).T)

    nc = bacc.Bacc("TRN2", target_bir_lowering=False, num_devices=1)
    arrays, args = {}, []
    consts = {"window": window, "ident": ident, "order": order}
    for name in _INS + list(consts):
        a = np.ascontiguousarray(consts[name] if name in consts else inputs[name])
        arrays[f"in_{name}"] = a
        args.append(nc.dram_tensor(f"in_{name}", a.shape, mybir.dt.from_np(a.dtype), kind="ExternalInput").ap())
    out = nc.dram_tensor("out", (BATCH, TOK, HID), F32, kind="ExternalOutput").ap()
    audio_tower(nc, *args, out)
    r = run_bass_kernel_spmd(nc, [arrays], core_ids=[0])
    return r.results[0]["out"]
```

```python
from contextlib import ExitStack

import concourse.bass as bass
from concourse import mybir

F32 = mybir.dt.float32
BF16 = mybir.dt.bfloat16
ALU = mybir.AluOpType
ACT = mybir.ActivationFunctionType
AX = mybir.AxisListType

BATCH, SAMPLES = 64, 4000
FRAME, HOP, HID = 256, 64, 256
HEADS, HD = 16, 16
EXPERTS, CAPACITY = 8, 100
TOK = (SAMPLES - FRAME) // HOP + 1
BLOCKS = TOK + 2
PAIRS = BATCH // 2
HALF = 64
P = 128
KC = HID // P
HG = HEADS // KC
HP = HEADS // 2
EPS = 1e-5


class Pair:

    def __init__(self, i, c):
        self.static = isinstance(i, int)
        self.i, self.c = i, c
        self.n = UNROLL * i + c
        self.par = c % 2
        self.half = UNROLL // 2 * i + c // 2

    def exists(self):
        return not self.static or 0 <= self.n < PAIRS

    def __add__(self, k):
        return Pair(self.i, self.c + k)

    def __sub__(self, k):
        return Pair(self.i, self.c - k)


UNROLL = 2
LOOP_FROM, LOOP_TO = 6, PAIRS - 6
FIRST_STEP, LAST_STEP = -6, PAIRS + 1


def steps(eng, step):
    for t in range(FIRST_STEP, LOOP_FROM):
        step(Pair(0, t))
    with eng.Fori(0, (LOOP_TO - LOOP_FROM) // UNROLL) as i:
        for k in range(UNROLL):
            step(Pair(i, LOOP_FROM + k))
    for t in range(LOOP_TO, LAST_STEP + 1):
        step(Pair(0, t))


def after(eng, sem, pair, each=1):
    if pair.exists():
        eng.wait_ge(sem, (pair.n + 1) * each)


def after_latest(eng, *events):
    for sem, pair, each in events:
        if pair.exists():
            after(eng, sem, pair, each)
            return


def after_dma(eng, sems, pair, count):
    if pair.exists():
        eng.wait_ge(sems[pair.par], (pair.half + 1) * 16 * count)


def audio_tower(nc, x, tok_w, tok_b, w_qkv, b_qkv, w_out, b_out, w_gate, w_expert, b_expert,
                window, ident_in, order_in, out):
    with ExitStack() as ctx:
        def sb(name, shape, dt=F32):
            return ctx.enter_context(nc.sbuf_tensor(name, shape, dt))

        def ps(name, shape, dt=F32):
            return ctx.enter_context(nc.psum_tensor(name, shape, dt))

        def sem(name):
            return ctx.enter_context(nc.semaphore(name))

        ident = sb("ident", [P, P])
        order_f = sb("order_f", [P, 2 * P + EXPERTS])
        order = sb("order", [P, 2 * P], BF16)
        rank = order_f[:, 2 * P:2 * P + EXPERTS]
        win = sb("win", [P, KC])
        wtok = sb("wtok", [P, KC, HID])
        wqkv = sb("wqkv", [P, KC, 3 * HID])
        wout = sb("wout", [P, KC, HID])
        wffn = sb("wffn", [P, KC, HID + EXPERTS])
        tokb = sb("tokb", [P, HID])
        expb = sb("expb", [P, HID])
        outb = sb("outb", [P, HID])
        qkvb = sb("qkvb", [P, 3 * KC])
        qkb, vb = qkvb[:, 0:2 * KC], qkvb[:, 2 * KC:3 * KC]
        vb_wide = sb("vb_wide", [P, KC, P])
        sums_of = sb("sums_of", [P, 2 * HD])
        eps = sb("eps", [P, 1])
        half_exp = sb("half_exp", [P, 1])
        blk = [sb(f"blk{j}", [P, P]) for j in range(2)]
        blkT = [sb(f"blkT{j}", [P, P + 4]) for j in range(2)]
        h = [sb(f"h{j}", [P, HID]) for j in range(2)]
        xn = [sb(f"xn{j}", [P, HID]) for j in range(2)]
        xnT = [sb(f"xnT{j}", [P, KC, P]) for j in range(2)]
        qk = [sb(f"qk{j}", [P, 2 * KC, P]) for j in range(2)]
        kdiag = [sb(f"kdiag{j}", [P, KC * 2, HG, TOK]) for j in range(2)]
        vdiag = [sb(f"vdiag{j}", [P, 2, HP, 2 * HD]) for j in range(2)]
        top = [sb(f"top{j}", [P, HEADS]) for j in range(2)]
        shifted = [sb(f"shifted{j}", [P, HEADS, TOK]) for j in range(2)]
        prob = [sb(f"prob{j}", [P, HEADS, HALF]) for j in range(2)]
        probT = [sb(f"probT{j}", [P, HP, P]) for j in range(2)]
        rsum = [sb(f"rsum{j}", [P, KC, P]) for j in range(2)]
        attT = [sb(f"attT{j}", [P, KC, P]) for j in range(2)]
        h2 = [sb(f"h2_{j}", [P, HID]) for j in range(2)]
        xn2 = [sb(f"xn2_{j}", [P, HID]) for j in range(2)]
        xn2T = [sb(f"xn2T{j}", [P, KC, P]) for j in range(2)]
        y_raw = [sb(f"y_raw{j}", [P, HID + EXPERTS]) for j in range(2)]
        y = [sb(f"y{j}", [P, HID]) for j in range(2)]
        res = [sb(f"res{j}", [P, HID]) for j in range(2)]
        stat = [[sb(f"stat{l}_{j}", [P, 6]) for j in range(2)] for l in range(2)]
        mv = [[sb(f"mv{l}_{j}", [P, 2]) for j in range(2)] for l in range(2)]
        veps = [[sb(f"veps{l}_{j}", [P, 1]) for j in range(2)] for l in range(2)]
        rstd = [[sb(f"rstd{l}_{j}", [P, 1]) for j in range(2)] for l in range(2)]
        resid = sb("resid", [P, PAIRS * HID])
        gtop = [sb(f"gtop{j}", [P, 1]) for j in range(2)]
        glog = [sb(f"glog{j}", [P, EXPERTS]) for j in range(2)]
        gexp = [sb(f"gexp{j}", [P, EXPERTS]) for j in range(2)]
        gsum = [sb(f"gsum{j}", [P, 1]) for j in range(2)]
        gate = [sb(f"gate{j}", [P, 1]) for j in range(2)]
        ghit = [sb(f"ghit{j}", [P, EXPERTS]) for j in range(2)]
        gbest = [sb(f"gbest{j}", [P, 1]) for j in range(2)]
        mask = [sb(f"mask{j}", [P, EXPERTS], BF16) for j in range(2)]
        place = [sb(f"place{j}", [P, EXPERTS]) for j in range(2)]
        keep8 = [sb(f"keep8_{j}", [P, EXPERTS]) for j in range(2)]
        kept = [sb(f"kept{j}", [P, 1]) for j in range(2)]
        weight = [sb(f"weight{j}", [P, 1]) for j in range(2)]
        carry = sb("carry", [P, EXPERTS])

        ps_s = ps("ps_s", [P, KC, 512])
        ps_pT = ps("ps_pT", [P, HP, P])
        ps_qk = ps("ps_qk", [P, 2 * KC, P])
        ps_t = ps("ps_t", [P, 512])
        ps_p = ps("ps_p", [P, 512])
        ps_o = ps("ps_o", [P, 2, KC, P])

        s_w_tok = sem("s_w_tok")
        s_w_qkv = sem("s_w_qkv")
        s_w_out = sem("s_w_out")
        s_w_ffn = sem("s_w_ffn")
        s_blocks = [sem(f"s_blocks{j}") for j in range(2)]
        s_kdiag = [sem(f"s_kdiag{j}") for j in range(2)]
        s_stored = [sem(f"s_stored{j}") for j in range(2)]
        s_zeroed = sem("s_zeroed")
        s_wtok = sem("s_wtok")
        s_order = sem("s_order")
        s_vb_wide = sem("s_vb_wide")
        s_vb_mm = sem("s_vb_mm")
        s_outb = sem("s_outb")
        blkT_done = sem("blkT_done")
        tok_done = sem("tok_done")
        xnT_done = sem("xnT_done")
        qk_done = sem("qk_done")
        v_done = sem("v_done")
        score_done = sem("score_done")
        pT_done = sem("pT_done")
        pv_done = sem("pv_done")
        out_done = sem("out_done")
        xn2T_done = sem("xn2T_done")
        ffn_done = sem("ffn_done")
        count_done = sem("count_done")
        blkT_ready = sem("blkT_ready")
        xnT_ready = sem("xnT_ready")
        v_ready = sem("v_ready")
        prob_ready = sem("prob_ready")
        pT_ready = sem("pT_ready")
        xn2T_ready = sem("xn2T_ready")
        gsum_ready = sem("gsum_ready")
        qk_ready = sem("qk_ready")
        y_raw_ready = sem("y_raw_ready")
        h_ready = sem("h_ready")
        stat_ready = [sem(f"stat_ready{l}") for l in range(2)]
        mv_ready = [sem(f"mv_ready{l}") for l in range(2)]
        xn_ready = sem("xn_ready")
        top_ready = sem("top_ready")
        shifted_ready = sem("shifted_ready")
        rsum_ready = sem("rsum_ready")
        att_ready = sem("att_ready")
        h2_ready = sem("h2_ready")
        xn2_ready = sem("xn2_ready")
        gtop_ready = sem("gtop_ready")
        glog_ready = sem("glog_ready")
        ghit_ready = sem("ghit_ready")
        gbest_ready = sem("gbest_ready")
        mask_ready = sem("mask_ready")
        gate_ready = sem("gate_ready")
        place_ready = sem("place_ready")
        kept_ready = sem("kept_ready")
        weight_ready = sem("weight_ready")
        carry_ready = sem("carry_ready")
        res_ready = sem("res_ready")
        veps_ready = [sem(f"veps_ready{l}") for l in range(2)]
        rstd_ready = [sem(f"rstd_ready{l}") for l in range(2)]
        resid_ready = sem("resid_ready")
        y_ready = sem("y_ready")

        block = ctx.enter_context(nc.Block())

        def row(v):
            return bass.AP(tensor=v.tensor, offset=v.offset, ap=[[0, P], [1, v.shape[0]]])

        @block.sync
        def _(sp):
            loads = [
                (s_w_tok, wtok[:], tok_w.rearrange("(c p) n -> p c n", p=P)),
                (s_w_tok, ident[:], ident_in),
                (s_w_tok, win[:], window),
                (s_w_tok, tokb[:], row(tok_b)),
                (s_w_qkv, wqkv[:], w_qkv.rearrange("(c p) n -> p c n", p=P)),
                (s_w_qkv, qkvb[:], b_qkv),
                (s_w_out, wout[:], w_out.rearrange("(c p) n -> p c n", p=P)),
                (s_w_out, outb[:], row(b_out)),
                (s_w_ffn, wffn[:, :, 0:HID], w_expert.rearrange("(c p) n -> p c n", p=P)),
                (s_w_ffn, wffn[:, :, HID:], w_gate.rearrange("(c p) n -> p c n", p=P)),
                (s_w_ffn, expb[:], row(b_expert)),
                (s_w_ffn, order_f[:], order_in),
            ]

            def load_blocks(u):
                after(sp, blkT_done, u - 2)
                for b in range(2):
                    src = x[0:1, 0:P]
                    src = bass.AP(tensor=src.tensor, offset=(2 * u.n + b) * SAMPLES, ap=[[HOP, BLOCKS], [1, P]])
                    sp.dma_start(blk[u.par][HALF * b:HALF * b + BLOCKS, :], src).then_inc(s_blocks[u.par], 16)

            def spread_k(u):
                after(sp, qk_ready, u, 2 * KC)
                for hh in range(HG):
                    rows = slice(HD * hh, HD * hh + HD)
                    src = qk[u.par][rows, KC:2 * KC, :].rearrange("p c (b n) -> p (c b) n", b=2)[:, :, 0:TOK]
                    sp.dma_start(kdiag[u.par][rows, :, hh, :], src).then_inc(s_kdiag[u.par], 16)

            def store(u):
                after(sp, res_ready, u)
                for b in range(2):
                    dst = bass.AP(tensor=out.tensor, offset=(2 * u.n + b) * TOK * HID, ap=[[HID, TOK], [1, HID]])
                    sp.dma_start(dst, res[u.par][HALF * b:HALF * b + TOK, :]).then_inc(s_stored[u.par], 16)

            sp.wait_ge(s_zeroed, 1)
            first = True

            def step(t):
                nonlocal first
                if (t - 2).exists():
                    store(t - 2)
                if (t + 2).exists():
                    if t.static and t.n == -2:
                        sp.wait_ge(s_zeroed, 2)
                    spread_k(t + 2)
                if (t + 6).exists():
                    load_blocks(t + 6)
                if first:
                    for landed, dst, src in loads:
                        sp.dma_start(dst, src).then_inc(landed, 16)
                    first = False

            steps(sp, step)
            for j in range(2):
                sp.wait_ge(s_stored[j], PAIRS // 2 * 2 * 16)

        @block.gpsimd
        def _(pool):
            for t_ in blk:
                last = nc.gpsimd.memset(t_[:], 0.0)
            last.then_inc(s_zeroed, 1)
            for t_ in kdiag:
                last = nc.gpsimd.memset(t_[:], 0.0)
            last.then_inc(s_zeroed, 1)
            nc.gpsimd.memset(eps[:], EPS)
            nc.gpsimd.memset(half_exp[:], -0.5)
            for t_ in blkT + vdiag + prob + attT + [carry, sums_of]:
                last = nc.gpsimd.memset(t_[:], 0.0)
            last.then_inc(s_zeroed, 1)
            pool.wait_ge(s_zeroed, 3)

            def inverse_deviation(l, u):
                after(pool, mv_ready[l], u)
                nc.gpsimd.tensor_tensor(veps[l][u.par][:], mv[l][u.par][:, 1:2], eps[:], ALU.add).then_inc(veps_ready[l], 1)
                after(pool, veps_ready[l], u)
                nc.gpsimd.tensor_tensor(rstd[l][u.par][:], veps[l][u.par][:], half_exp[:], ALU.pow).then_inc(rstd_ready[l], 1)

            def attention_residual(u):
                if u.static and u.n == 0:
                    pool.wait_ge(s_outb, 1)
                after(pool, h_ready, u)
                nc.gpsimd.tensor_tensor(resid[:, bass.ds(u.n * HID, HID)], h[u.par][:], outb[:], ALU.add).then_inc(resid_ready, 1)

            def expert_bias(u):
                after(pool, y_raw_ready, u)
                after(pool, res_ready, u - 2)
                nc.gpsimd.tensor_tensor(y[u.par][:], y_raw[u.par][:, 0:HID], expb[:], ALU.add).then_inc(y_ready, 1)

            def step(t):
                if (t - 2).exists():
                    expert_bias(t - 2)
                if (t - 1).exists():
                    inverse_deviation(1, t - 1)
                if (t + 3).exists():
                    inverse_deviation(0, t + 3)
                    attention_residual(t + 3)

            steps(pool, step)

        @block.scalar
        def _(act):
            act.wait_ge(s_zeroed, 3)

            def transposed_xn2(u):
                after(act, xn2T_done, u)
                after(act, ffn_done, u - 2)
                nc.scalar.copy(xn2T[u.par][:], ps_t[:, 0:HID]).then_inc(xn2T_ready, 1)

            def exponentials(u):
                after(act, pT_done, u - 2, KC)
                for g in range(KC):
                    act.wait_ge(shifted_ready, u.n * KC + g + 1)
                    part = slice(g * HG, (g + 1) * HG)
                    nc.scalar.activation(prob[u.par][:, part, 0:TOK], shifted[u.par][:, part, :], ACT.Exp).then_inc(prob_ready, 1)

            def values(u):
                after(act, v_done, u)
                after(act, pv_done, u - 2)
                for r in range(2):
                    rows = slice(HALF * r, HALF * r + HALF)
                    nc.scalar.copy(vdiag[u.par][rows, :, :, HD * r:HD * r + HD],
                                   ps_t[rows, 0:HID].rearrange("k (b p d) -> k b p d", b=2, d=HD)).then_inc(v_ready, 1)

            def queries_keys(u):
                after(act, qk_done, u)
                after(act, score_done, u - 2)
                after_dma(act, s_kdiag, u - 2, HG)
                for m in range(2 * KC):
                    nc.scalar.activation(qk[u.par][:, m, :], ps_qk[:, m, :], ACT.Identity, bias=qkb[:, m:m + 1]).then_inc(qk_ready, 1)

            def expert(u):
                after(act, ffn_done, u)
                after(act, y_ready, u - 2)
                after(act, glog_ready, u - 2)
                nc.scalar.copy(y_raw[u.par][:], ps_p[:, 0:HID + EXPERTS]).then_inc(y_raw_ready, 1)

            def gate_sum(u):
                after(act, glog_ready, u)
                nc.scalar.activation(gexp[u.par][:], glog[u.par][:], ACT.Exp, accum_out=gsum[u.par][:]).then_inc(gsum_ready, 1)

            def transposed_blocks(u):
                after(act, blkT_done, u)
                after(act, tok_done, u - 2)
                nc.scalar.copy(blkT[u.par][:, 0:P], ps_t[:, 0:P]).then_inc(blkT_ready, 1)

            def transposed_probs(u):
                after(act, pv_done, u - 2)
                for g in range(KC):
                    if u.exists():
                        act.wait_ge(pT_done, u.n * KC + g + 1)
                    part = slice(g * HP // KC, (g + 1) * HP // KC)
                    nc.scalar.copy(probT[u.par][:, part, :], ps_pT[:, part, :]).then_inc(pT_ready, 1)

            def transposed_xn(u):
                after(act, xnT_done, u)
                after(act, v_done, u - 2)
                nc.scalar.copy(xnT[u.par][:], ps_t[:, 0:HID]).then_inc(xnT_ready, 1)

            def step(t):
                if (t + 2).exists():
                    transposed_xn(t + 2)
                if (t - 2).exists():
                    expert(t - 2)
                if t.exists():
                    exponentials(t)
                if (t + 1).exists():
                    values(t + 1)
                if (t - 2).exists():
                    gate_sum(t - 2)
                if t.exists():
                    transposed_probs(t)
                if (t + 2).exists():
                    queries_keys(t + 2)
                if (t + 4).exists():
                    transposed_blocks(t + 4)
                if (t - 1).exists():
                    transposed_xn2(t - 1)

            steps(act, step)

        @block.vector
        def _(dve):
            def window_weights():
                dve.wait_ge(s_w_tok, 4 * 16)
                for c in range(KC):
                    nc.vector.tensor_scalar(wtok[:, c, :], wtok[:, c, :], win[:, c:c + 1], None, ALU.mult).then_inc(s_wtok, 1)

            def value_bias():
                dve.wait_ge(s_w_qkv, 2 * 16)
                dve.wait_ge(s_zeroed, 3)
                for c in range(KC):
                    nc.vector.tensor_scalar(vb_wide[:, c, :], vb[:, c:c + 1].to_broadcast([P, P]), 1.0 / HID ** 0.5, None, ALU.mult).then_inc(s_vb_wide, 1)
                for r in range(2):
                    last = nc.vector.memset(sums_of[HALF * r:HALF * r + TOK, HD * r:HD * r + HD], HID ** 0.5)
                last.then_inc(s_vb_wide, 1)

            def output_bias():
                dve.wait_ge(s_w_out, 2 * 16)
                dve.wait_ge(s_vb_mm, 1)
                nc.vector.tensor_tensor(outb[:], ps_p[:, 0:HID], outb[:], ALU.add).then_inc(s_outb, 1)

            def token_order():
                dve.wait_ge(s_w_ffn, 4 * 16)
                nc.vector.tensor_copy(order[:], order_f[:, 0:2 * P]).then_inc(s_order, 1)

            def aggregate(l, u):
                nc.vector.bn_aggr(mv[l][u.par][:], stat[l][u.par][:]).then_inc(mv_ready[l], 1)

            def residual(u):
                after(dve, res_ready, u - 2)
                after(dve, out_done, u)
                after(dve, resid_ready, u)
                nc.vector.tensor_tensor(h2[u.par][:], ps_p[:, 0:HID], resid[:, bass.ds(u.n * HID, HID)], ALU.add).then_inc(h2_ready, 1)
                after(dve, h2_ready, u)
                nc.vector.bn_stats(stat[1][u.par][:], h2[u.par][:]).then_inc(stat_ready[1], 1)

            def normalize2(u):
                after(dve, rstd_ready[1], u)
                after(dve, xn2T_done, u - 2)
                nc.vector.tensor_scalar(xn2[u.par][:], h2[u.par][:], mv[1][u.par][:, 0:1], rstd[1][u.par][:], ALU.subtract, ALU.mult).then_inc(xn2_ready, 1)

            def gate_value(u):
                after(dve, gsum_ready, u)
                nc.vector.reciprocal(gate[u.par][:], gsum[u.par][:]).then_inc(gate_ready, 1)

            def queue_places(u):
                j = u.par
                after(dve, count_done, u)
                after(dve, carry_ready, u - 1)
                nc.vector.tensor_tensor(place[j][:], ps_qk[:, 0, 0:EXPERTS], carry[:], ALU.add).then_inc(place_ready, 1)
                nc.vector.tensor_tensor(carry[:], ps_qk[:, 0, EXPERTS:2 * EXPERTS], carry[:], ALU.add).then_inc(carry_ready, 1)

            def gate_weight(u):
                j = u.par
                after(dve, place_ready, u)
                nc.vector.scalar_tensor_tensor(keep8[j][:], place[j][:], float(CAPACITY), mask[j][:], ALU.is_le, ALU.mult,
                                               accum_out=kept[j][:]).then_inc(kept_ready, 1)
                after(dve, kept_ready, u)
                after(dve, gate_ready, u)
                nc.vector.tensor_tensor(weight[j][:], kept[j][:], gate[j][:], ALU.mult).then_inc(weight_ready, 1)

            def result(u):
                after(dve, weight_ready, u)
                after(dve, y_ready, u)
                after_dma(dve, s_stored, u - 2, 2)
                nc.vector.scalar_tensor_tensor(res[u.par][:], y[u.par][:], weight[u.par][:], h2[u.par][:], ALU.mult, ALU.add).then_inc(res_ready, 1)

            def maximum(u):
                after(dve, score_done, u)
                nc.vector.tensor_reduce(top[u.par][:].rearrange("q (g h) -> q g h", g=KC),
                                        ps_s[:, :, 0:HG * TOK].rearrange("q g (h k) -> q g h k", h=HG), AX.X, ALU.max).then_inc(top_ready, 1)
                after(dve, top_ready, u)
                after(dve, prob_ready, u - 2, KC)

            def shift(u, g):
                part = slice(g * HG, (g + 1) * HG)
                nc.vector.tensor_tensor(shifted[u.par][:, part, :], ps_s[:, g, 0:HG * TOK].rearrange("q (h k) -> q h k", h=HG),
                                        top[u.par][:, part].unsqueeze(2).to_broadcast([P, HG, TOK]), ALU.subtract).then_inc(shifted_ready, 1)

            def logits(u):
                j = u.par
                after(dve, y_raw_ready, u)
                nc.vector.tensor_reduce(gtop[j][:], y_raw[j][:, HID:], AX.X, ALU.max).then_inc(gtop_ready, 1)
                after(dve, gtop_ready, u)
                nc.vector.tensor_scalar(glog[j][:], y_raw[j][:, HID:], gtop[j][:], None, ALU.subtract).then_inc(glog_ready, 1)

            def best_expert(u):
                j = u.par
                after(dve, glog_ready, u)
                nc.vector.scalar_tensor_tensor(ghit[j][:], glog[j][:], 0.0, rank, ALU.is_ge, ALU.mult).then_inc(ghit_ready, 1)
                after(dve, ghit_ready, u)
                nc.vector.tensor_reduce(gbest[j][:], ghit[j][:], AX.X, ALU.max).then_inc(gbest_ready, 1)
                after(dve, gbest_ready, u)
                nc.vector.tensor_scalar(mask[j][:], rank, gbest[j][:], None, ALU.is_equal).then_inc(mask_ready, 1)



            def tokens(u):
                after(dve, tok_done, u)
                after(dve, resid_ready, u - 2)
                nc.vector.tensor_tensor(h[u.par][:], ps_p[:, 0:HID], tokb[:], ALU.add).then_inc(h_ready, 1)
                after(dve, h_ready, u)
                nc.vector.bn_stats(stat[0][u.par][:], h[u.par][:]).then_inc(stat_ready[0], 1)

            def normalize(u):
                after(dve, rstd_ready[0], u)
                after(dve, xnT_done, u - 2)
                nc.vector.tensor_scalar(xn[u.par][:], h[u.par][:], mv[0][u.par][:, 0:1], rstd[0][u.par][:], ALU.subtract, ALU.mult).then_inc(xn_ready, 1)

            def real_tokens(a):
                return a.rearrange("f c (b n) -> f c b n", b=2)[:, :, :, 0:TOK]

            def inverse_sums(u):
                after(dve, pv_done, u)
                nc.vector.reciprocal(real_tokens(rsum[u.par][:]), real_tokens(ps_o[:, 1, :, :])).then_inc(rsum_ready, 1)

            def attention_out(u):
                after(dve, rsum_ready, u)
                after(dve, out_done, u - 2)
                nc.vector.tensor_tensor(real_tokens(attT[u.par][:]), real_tokens(ps_o[:, 0, :, :]), real_tokens(rsum[u.par][:]), ALU.mult).then_inc(att_ready, 1)

            def step(t):
                if t.static and t.n == -2:
                    value_bias()
                if t.static and t.n == -1:
                    output_bias()
                    token_order()
                if (t + 2).exists():
                    normalize(t + 2)
                if (t - 1).exists():
                    inverse_sums(t - 1)
                    attention_out(t - 1)
                if t.exists():
                    maximum(t)
                    shift(t, 0)
                    shift(t, 1)
                if (t - 2).exists():
                    logits(t - 2)
                if (t - 1).exists():
                    residual(t - 1)
                    after(dve, stat_ready[1], t - 1)
                if (t - 2).exists():
                    best_expert(t - 2)
                if (t - 1).exists():
                    aggregate(1, t - 1)
                if (t + 3).exists():
                    tokens(t + 3)
                if (t - 1).exists():
                    normalize2(t - 1)
                if (t + 3).exists():
                    after(dve, stat_ready[0], t + 3)
                if (t - 2).exists():
                    gate_value(t - 2)
                if (t + 3).exists():
                    aggregate(0, t + 3)
                if (t - 2).exists():
                    queue_places(t - 2)
                    gate_weight(t - 2)
                    result(t - 2)

            window_weights()
            steps(dve, step)

        @block.tensor
        def _(pe):
            pe.wait_ge(s_w_tok, 4 * 16)
            pe.wait_ge(s_wtok, KC)

            def output_bias():
                pe.wait_ge(s_w_out, 2 * 16)
                pe.wait_ge(s_vb_wide, KC + 1)
                pe.wait_ge(h_ready, 2)
                for c in range(KC):
                    last = nc.tensor.matmul(ps_p[:, 0:HID], vb_wide[:, c, :], wout[:, c, :], start=(c == 0), stop=(c == KC - 1))
                last.then_inc(s_vb_mm, 1)
                pe.wait_ge(s_outb, 1)
                pe.wait_ge(s_order, 1)

            def transpose_blocks(u):
                after_dma(pe, s_blocks, u, 2)
                after_latest(pe, (v_ready, u - 3, 2), (xnT_ready, u - 2, 1), (blkT_ready, u - 1, 1))
                nc.tensor.transpose(ps_t[:, 0:P], blk[u.par][:], ident[:]).then_inc(blkT_done, 1)

            def tokens(u):
                after(pe, blkT_ready, u)
                after_latest(pe, (h2_ready, u - 4, 1), (h_ready, u - 1, 1))
                for c in range(KC):
                    last = nc.tensor.matmul(ps_p[:, 0:HID], blkT[u.par][:, 2 * c:2 * c + P], wtok[:, c, :], start=(c == 0), stop=(c == KC - 1))
                last.then_inc(tok_done, 1)

            def transpose_xn(u):
                after(pe, xn_ready, u)
                after_latest(pe, (xn2T_ready, u - 4, 1), (blkT_ready, u + 1, 1))
                for c in range(KC):
                    last = nc.tensor.transpose(ps_t[:, P * c:P * c + P], xn[u.par][:, P * c:P * c + P], ident[:])
                last.then_inc(xnT_done, 1)

            def queries_keys(u):
                after(pe, xnT_ready, u)
                after_latest(pe, (carry_ready, u - 5, 1), (qk_ready, u - 1, 2 * KC))
                for m in range(2 * KC):
                    for c in range(KC):
                        last = nc.tensor.matmul(ps_qk[:, m, :], wqkv[:, c, P * m:P * m + P], xnT[u.par][:, c, :], start=(c == 0), stop=(c == KC - 1))
                last.then_inc(qk_done, 1)

            def values(u):
                after_latest(pe, (xnT_ready, u + 1, 1), (xn2T_ready, u - 3, 1))
                for b in range(2):
                    for c in range(KC):
                        for r in range(2):
                            w = wqkv[:, c, 2 * HID:3 * HID].rearrange("f (p r d) -> f r p d", r=2, d=HD)[:, r]
                            last = nc.tensor.matmul(ps_t[HALF * r:HALF * r + HALF, P * b:P * b + P],
                                                    xnT[u.par][:, c, HALF * b:HALF * b + HALF], w,
                                                    start=(c == 0), stop=(c == KC - 1))
                last.then_inc(v_done, 1)

            def scores(u):
                after_dma(pe, s_kdiag, u, HG)
                after(pe, qk_ready, u, 2 * KC)
                after(pe, shifted_ready, u - 1, KC)
                for g in range(KC):
                    for b in range(2):
                        last = nc.tensor.matmul(ps_s[HALF * b:HALF * b + HALF, g, 0:HG * TOK],
                                                qk[u.par][:, g, HALF * b:HALF * b + HALF],
                                                kdiag[u.par][:, 2 * g + b, :, :].rearrange("p h k -> p (h k)"), start=True, stop=True)
                last.then_inc(score_done, 1)

            def transpose_probs(u):
                after(pe, pT_ready, u - 1, KC)
                for p in range(HP):
                    if p % (HP // KC) == 0:
                        pe.wait_ge(prob_ready, u.n * KC + p // (HP // KC) + 1)
                    last = nc.tensor.transpose(ps_pT[:, p, :], prob[u.par][:, 2 * p:2 * p + 2, :].rearrange("q h k -> q (h k)"), ident[:])
                    if p % (HP // KC) == HP // KC - 1:
                        last.then_inc(pT_done, 1)

            def weighted_values(u):
                after(pe, v_ready, u, 2)
                after(pe, att_ready, u - 1)
                quads = HP // KC
                for g in range(KC):
                    pe.wait_ge(pT_ready, u.n * KC + g + 1)
                    for b in range(2):
                        for c in range(quads):
                            p = g * quads + c
                            nc.tensor.matmul(ps_o[2 * HD * c:2 * HD * (c + 1), 0, g, HALF * b:HALF * b + HALF],
                                             vdiag[u.par][:, b, p, :], probT[u.par][:, p, HALF * b:HALF * b + HALF], start=True, stop=True)
                for c in range(quads):
                    last = nc.tensor.matmul(ps_o[2 * HD * c:2 * HD * (c + 1), 1, :, :], sums_of[:], probT[u.par][:, c::quads, :], start=True, stop=True)
                last.then_inc(pv_done, 1)

            def project(u):
                after(pe, att_ready, u)
                after_latest(pe, (y_raw_ready, u - 1, 1), (h_ready, u + 3, 1))
                for c in range(KC):
                    last = nc.tensor.matmul(ps_p[:, 0:HID], attT[u.par][:, c, :], wout[:, c, :], start=(c == 0), stop=(c == KC - 1))
                last.then_inc(out_done, 1)

            def transpose_xn2(u):
                after(pe, xn2_ready, u)
                after_latest(pe, (blkT_ready, u + 5, 1), (v_ready, u + 2, 2), (xn2T_ready, u - 1, 1))
                for c in range(KC):
                    last = nc.tensor.transpose(ps_t[:, P * c:P * c + P], xn2[u.par][:, P * c:P * c + P], ident[:])
                last.then_inc(xn2T_done, 1)

            def expert(u):
                after(pe, xn2T_ready, u)
                after_latest(pe, (h_ready, u + 4, 1), (h2_ready, u, 1))
                for c in range(KC):
                    last = nc.tensor.matmul(ps_p[:, 0:HID + EXPERTS], xn2T[u.par][:, c, :], wffn[:, c, :], start=(c == 0), stop=(c == KC - 1))
                last.then_inc(ffn_done, 1)

            def counts(u):
                after(pe, mask_ready, u)
                after_latest(pe, (qk_ready, u + 4, 2 * KC), (carry_ready, u - 1, 1))
                for c in range(2):
                    last = nc.tensor.matmul(ps_qk[:, 0, EXPERTS * c:EXPERTS * (c + 1)], order[:, P * c:P * c + P], mask[u.par][:], start=True, stop=True)
                last.then_inc(count_done, 1)

            def step(t):
                if t.static and t.n == -2:
                    pe.wait_ge(s_w_qkv, 2 * 16)
                if t.static and t.n == -1:
                    output_bias()
                if t.exists():
                    scores(t)
                if (t + 2).exists():
                    transpose_xn(t + 2)
                if (t - 2).exists():
                    expert(t - 2)
                if (t + 2).exists():
                    queries_keys(t + 2)
                if (t - 1).exists():
                    project(t - 1)
                if (t + 1).exists():
                    values(t + 1)
                if t.exists():
                    transpose_probs(t)
                if (t + 3).exists():
                    tokens(t + 3)
                if (t + 4).exists():
                    transpose_blocks(t + 4)
                if t.exists():
                    weighted_values(t)
                if (t - 2).exists():
                    counts(t - 2)
                if (t - 1).exists():
                    transpose_xn2(t - 1)

            steps(pe, step)


_INS = ["x", "L0_tok_W", "L0_tok_b", "L0_attn_W_qkv", "L0_attn_b_qkv", "L0_attn_W_out", "L0_attn_b_out",
        "L0_ffn_w_gate", "L0_ffn_w_expert", "L0_ffn_b_expert"]


def kernel(**inputs):
    import numpy as np
    import concourse.bacc as bacc
    from concourse.bass_utils import run_bass_kernel_spmd

    window = np.hanning(FRAME).astype(np.float32).reshape(KC, P).T
    ident = np.eye(P, dtype=np.float32)
    real = (np.arange(P) % HALF < TOK)[:, None]
    upto = np.arange(P)[:, None] <= np.arange(P)[None, :]
    rank = np.broadcast_to(EXPERTS - np.arange(EXPERTS), (P, EXPERTS))
    order = np.concatenate([upto & real, np.broadcast_to(real, (P, P)), rank], 1).astype(np.float32)

    inputs = dict(inputs, L0_attn_b_qkv=np.asarray(inputs["L0_attn_b_qkv"]).reshape(3 * KC, P).T)

    nc = bacc.Bacc("TRN2", target_bir_lowering=False, num_devices=1)
    arrays, args = {}, []
    consts = {"window": window, "ident": ident, "order": order}
    for name in _INS + list(consts):
        a = np.ascontiguousarray(consts[name] if name in consts else inputs[name])
        arrays[f"in_{name}"] = a
        args.append(nc.dram_tensor(f"in_{name}", a.shape, mybir.dt.from_np(a.dtype), kind="ExternalInput").ap())
    out = nc.dram_tensor("out", (BATCH, TOK, HID), F32, kind="ExternalOutput").ap()
    audio_tower(nc, *args, out)
    r = run_bass_kernel_spmd(nc, [arrays], core_ids=[0])
    return r.results[0]["out"]
```

```python
from contextlib import ExitStack

import concourse.bass as bass
from concourse import mybir

F32 = mybir.dt.float32
BF16 = mybir.dt.bfloat16
F32R = mybir.dt.float32r
ALU = mybir.AluOpType
ACT = mybir.ActivationFunctionType
AX = mybir.AxisListType

BATCH, SAMPLES = 64, 4000
FRAME, HOP, HID = 256, 64, 256
HEADS, HD = 16, 16
EXPERTS, CAPACITY = 8, 100
TOK = (SAMPLES - FRAME) // HOP + 1
BLOCKS = TOK + 2
PAIRS = BATCH // 2
HALF = 64
P = 128
KC = HID // P
HG = HEADS // KC
HP = HEADS // 2
VW = 2 * HD + 2
EPS = 1e-5
WARM_UP = 10


class Pair:

    def __init__(self, i, c):
        self.static = isinstance(i, int)
        self.i, self.c = i, c
        self.n = UNROLL * i + c
        self.par = c % 2
        self.half = UNROLL // 2 * i + c // 2

    def exists(self):
        return not self.static or 0 <= self.n < PAIRS

    def __add__(self, k):
        return Pair(self.i, self.c + k)

    def __sub__(self, k):
        return Pair(self.i, self.c - k)


UNROLL = 2
LOOP_FROM, LOOP_TO = 6, PAIRS - 6
FIRST_STEP, LAST_STEP = -6, PAIRS + 2


def steps(eng, step):
    for t in range(FIRST_STEP, LOOP_FROM):
        step(Pair(0, t))
    with eng.Fori(0, (LOOP_TO - LOOP_FROM) // UNROLL) as i:
        for k in range(UNROLL):
            step(Pair(i, LOOP_FROM + k))
    for t in range(LOOP_TO, LAST_STEP + 1):
        step(Pair(0, t))


def after(eng, sem, pair, each=1):
    if pair.exists():
        eng.wait_ge(sem, (pair.n + 1) * each)


def after_latest(eng, *events):
    for sem, pair, each in events:
        if pair.exists():
            after(eng, sem, pair, each)
            return


def after_dma(eng, sems, pair, count):
    if pair.exists():
        eng.wait_ge(sems[pair.par], (pair.half + 1) * 16 * count)


def audio_tower(nc, x, tok_w, tok_b, w_qkv, b_qkv, w_out, b_out, w_gate, w_expert, b_expert,
                window, ident_in, order_in, out):
    with ExitStack() as ctx:
        def sb(name, shape, dt=F32):
            return ctx.enter_context(nc.sbuf_tensor(name, shape, dt))

        def ps(name, shape, dt=F32):
            return ctx.enter_context(nc.psum_tensor(name, shape, dt))

        def sem(name):
            return ctx.enter_context(nc.semaphore(name))

        ident = sb("ident", [P, P])
        order_f = sb("order_f", [P, 2 * P + EXPERTS])
        order = sb("order", [P, 2 * P], BF16)
        rank = order_f[:, 2 * P:2 * P + EXPERTS]
        warm = sb("warm", [P, 512], BF16)
        win = sb("win", [P, KC])
        wtok = sb("wtok", [P, KC, HID])
        wqkv = sb("wqkv", [P, KC, 3 * HID])
        wout = sb("wout", [P, KC, HID])
        wffn = sb("wffn", [P, KC, HID + EXPERTS])
        wtok_high, wtok_low = [sb(f"wtok_{part}", [P, KC, HID], F32R) for part in ("high", "low")]
        wv_high, wv_low = [sb(f"wv_{part}", [P, KC, HID], F32R) for part in ("high", "low")]
        wout_high, wout_low = [sb(f"wout_{part}", [P, KC, HID], F32R) for part in ("high", "low")]
        wffn_high, wffn_low = [sb(f"wffn_{part}", [P, KC, HID + EXPERTS], F32R) for part in ("high", "low")]
        tokb = sb("tokb", [P, HID])
        expb = sb("expb", [P, HID])
        outb = sb("outb", [P, HID])
        qkvb = sb("qkvb", [P, 3 * KC])
        qkb, vb = qkvb[:, 0:2 * KC], qkvb[:, 2 * KC:3 * KC]
        vb_wide = sb("vb_wide", [P, KC, P])
        eps = sb("eps", [P, 1])
        half_exp = sb("half_exp", [P, 1])
        eps_exp = sb("eps_exp", [P, 1])
        blk = [sb(f"blk{j}", [P, P]) for j in range(2)]
        blkT = [sb(f"blkT{j}", [P, P + 4], F32R) for j in range(2)]
        blkT_low = [sb(f"blkT_low{j}", [P, P + 4], F32R) for j in range(2)]
        h = [sb(f"h{j}", [P, HID]) for j in range(2)]
        xn = [sb(f"xn{j}", [P, HID]) for j in range(2)]
        xnT = [sb(f"xnT{j}", [P, KC, P]) for j in range(2)]
        xnT_high = [sb(f"xnT_high{j}", [P, KC, P], F32R) for j in range(2)]
        xnT_low = [sb(f"xnT_low{j}", [P, KC, P], F32R) for j in range(2)]
        v = [sb(f"v{j}", [P, HP, 2, HD]) for j in range(2)]
        qk = [sb(f"qk{j}", [P, 2 * KC, P]) for j in range(2)]
        kdiag = [sb(f"kdiag{j}", [P, KC * 2, HG, TOK]) for j in range(2)]
        vdiag = [sb(f"vdiag{j}", [P, 2, HP, VW]) for j in range(2)]
        top = [sb(f"top{j}", [P, HEADS]) for j in range(2)]
        shifted = [sb(f"shifted{j}", [P, HEADS, TOK]) for j in range(2)]
        prob = [sb(f"prob{j}", [P, HEADS, HALF]) for j in range(2)]
        probT = [sb(f"probT{j}", [P, HP, P]) for j in range(2)]
        rsum = [sb(f"rsum{j}", [P, HP, 2]) for j in range(2)]
        att = [sb(f"att{j}", [P, HID]) for j in range(2)]
        attT = [sb(f"attT{j}", [P, KC, P], F32R) for j in range(2)]
        attT_low = [sb(f"attT_low{j}", [P, KC, P], F32R) for j in range(2)]
        h2 = [sb(f"h2_{j}", [P, HID]) for j in range(2)]
        xn2 = [sb(f"xn2_{j}", [P, HID]) for j in range(2)]
        xn2T = [sb(f"xn2T{j}", [P, KC, P], F32R) for j in range(2)]
        xn2T_low = [sb(f"xn2T_low{j}", [P, KC, P], F32R) for j in range(2)]
        y_raw = [sb(f"y_raw{j}", [P, HID + EXPERTS]) for j in range(2)]
        y = [sb(f"y{j}", [P, HID]) for j in range(2)]
        res = [sb(f"res{j}", [P, HID]) for j in range(2)]
        stat = [[sb(f"stat{l}_{j}", [P, 6]) for j in range(2)] for l in range(2)]
        mv = [[sb(f"mv{l}_{j}", [P, 2]) for j in range(2)] for l in range(2)]
        veps = [[sb(f"veps{l}_{j}", [P, 1]) for j in range(2)] for l in range(2)]
        rstd = [[sb(f"rstd{l}_{j}", [P, 1]) for j in range(2)] for l in range(2)]
        resid = sb("resid", [P, PAIRS * HID])
        gtop = [sb(f"gtop{j}", [P, 1]) for j in range(2)]
        glog = [sb(f"glog{j}", [P, EXPERTS]) for j in range(2)]
        gexp = [sb(f"gexp{j}", [P, EXPERTS]) for j in range(2)]
        gsum = [sb(f"gsum{j}", [P, 1]) for j in range(2)]
        gate = [sb(f"gate{j}", [P, 1]) for j in range(2)]
        ghit = [sb(f"ghit{j}", [P, EXPERTS]) for j in range(2)]
        gbest = [sb(f"gbest{j}", [P, 1]) for j in range(2)]
        mask = [sb(f"mask{j}", [P, EXPERTS], BF16) for j in range(2)]
        place = [sb(f"place{j}", [P, EXPERTS]) for j in range(2)]
        keep8 = [sb(f"keep8_{j}", [P, EXPERTS]) for j in range(2)]
        kept = [sb(f"kept{j}", [P, 1]) for j in range(2)]
        weight = [sb(f"weight{j}", [P, 1]) for j in range(2)]
        carry = sb("carry", [P, EXPERTS])

        ps_s = ps("ps_s", [P, KC, 512])
        ps_pT = ps("ps_pT", [P, HP, P])
        ps_qk = ps("ps_qk", [P, 2 * KC, P])
        ps_t = ps("ps_t", [P, 512])
        ps_p = ps("ps_p", [P, 512])
        ps_o = ps("ps_o", [P, 512])
        ps_pv = ps_o[:, 0:HP * VW].rearrange("q (p v) -> q p v", p=HP)

        s_w_tok = sem("s_w_tok")
        s_w_qkv = sem("s_w_qkv")
        s_w_out = sem("s_w_out")
        s_w_ffn = sem("s_w_ffn")
        s_blocks = [sem(f"s_blocks{j}") for j in range(2)]
        s_kdiag = [sem(f"s_kdiag{j}") for j in range(2)]
        s_vdiag = [sem(f"s_vdiag{j}") for j in range(2)]
        s_stored = [sem(f"s_stored{j}") for j in range(2)]
        s_zeroed = sem("s_zeroed")
        s_kdiag_zeroed = sem("s_kdiag_zeroed")
        s_wtok = sem("s_wtok")
        s_wtok_split = sem("s_wtok_split")
        s_wv_split = sem("s_wv_split")
        s_wout_split = sem("s_wout_split")
        s_wffn_split = sem("s_wffn_split")
        s_warm = sem("s_warm")
        s_order = sem("s_order")
        s_vb_wide = sem("s_vb_wide")
        s_vb_mm = sem("s_vb_mm")
        s_outb = sem("s_outb")
        blkT_done = sem("blkT_done")
        tok_done = sem("tok_done")
        xnT_done = sem("xnT_done")
        qk_done = sem("qk_done")
        v_done = sem("v_done")
        score_done = sem("score_done")
        pT_done = sem("pT_done")
        pv_done = sem("pv_done")
        attT_done = sem("attT_done")
        out_done = sem("out_done")
        xn2T_done = sem("xn2T_done")
        ffn_done = sem("ffn_done")
        count_done = sem("count_done")
        blkT_ready = sem("blkT_ready")
        xnT_ready = sem("xnT_ready")
        xnT_high_ready = sem("xnT_high_ready")
        v_copied = sem("v_copied")
        v_ready = sem("v_ready")
        prob_ready = sem("prob_ready")
        pT_ready = sem("pT_ready")
        attT_ready = sem("attT_ready")
        xn2T_ready = sem("xn2T_ready")
        gsum_ready = sem("gsum_ready")
        k_ready = sem("k_ready")
        q_ready = sem("q_ready")
        y_raw_ready = sem("y_raw_ready")
        blkT_low_ready = sem("blkT_low_ready")
        attT_low_ready = sem("attT_low_ready")
        xn2T_low_ready = sem("xn2T_low_ready")
        h_ready = sem("h_ready")
        stat_ready = [sem(f"stat_ready{l}") for l in range(2)]
        mv_ready = [sem(f"mv_ready{l}") for l in range(2)]
        xn_ready = sem("xn_ready")
        top_ready = sem("top_ready")
        shifted_ready = sem("shifted_ready")
        rsum_ready = sem("rsum_ready")
        att_ready = sem("att_ready")
        h2_ready = sem("h2_ready")
        xn2_ready = sem("xn2_ready")
        gtop_ready = sem("gtop_ready")
        glog_ready = sem("glog_ready")
        ghit_ready = sem("ghit_ready")
        gbest_ready = sem("gbest_ready")
        mask_ready = sem("mask_ready")
        gate_ready = sem("gate_ready")
        place_ready = sem("place_ready")
        kept_ready = sem("kept_ready")
        weight_ready = sem("weight_ready")
        carry_ready = sem("carry_ready")
        res_ready = sem("res_ready")
        veps_ready = [sem(f"veps_ready{l}") for l in range(2)]
        rstd_ready = [sem(f"rstd_ready{l}") for l in range(2)]
        resid_ready = sem("resid_ready")
        y_ready = sem("y_ready")
        xnT_low_ready = sem("xnT_low_ready")

        block = ctx.enter_context(nc.Block())

        def row(v):
            return bass.AP(tensor=v.tensor, offset=v.offset, ap=[[0, P], [1, v.shape[0]]])

        @block.sync
        def _(sp):
            token_loads = [
                (s_w_tok, wtok[:], tok_w.rearrange("(c p) n -> p c n", p=P)),
                (s_w_tok, ident[:], ident_in),
                (s_w_tok, win[:], window),
                (s_w_tok, tokb[:], row(tok_b)),
            ]
            other_loads = [
                (s_w_qkv, wqkv[:], w_qkv.rearrange("(c p) n -> p c n", p=P)),
                (s_w_qkv, qkvb[:], b_qkv),
                (s_w_out, wout[:], w_out.rearrange("(c p) n -> p c n", p=P)),
                (s_w_out, outb[:], row(b_out)),
                (s_w_ffn, wffn[:, :, 0:HID], w_expert.rearrange("(c p) n -> p c n", p=P)),
                (s_w_ffn, wffn[:, :, HID:], w_gate.rearrange("(c p) n -> p c n", p=P)),
                (s_w_ffn, expb[:], row(b_expert)),
                (s_w_ffn, order_f[:], order_in),
            ]

            def load_blocks(u):
                after(sp, blkT_done, u - 2)
                for b in range(2):
                    src = x[0:1, 0:P]
                    src = bass.AP(tensor=src.tensor, offset=(2 * u.n + b) * SAMPLES, ap=[[HOP, BLOCKS], [1, P]])
                    sp.dma_start(blk[u.par][HALF * b:HALF * b + BLOCKS, :], src).then_inc(s_blocks[u.par], 16)

            def spread_k(u):
                after(sp, k_ready, u, KC)
                for hh in range(HG):
                    rows = slice(HD * hh, HD * hh + HD)
                    src = qk[u.par][rows, KC:2 * KC, :].rearrange("p c (b n) -> p (c b) n", b=2)[:, :, 0:TOK]
                    sp.dma_start(kdiag[u.par][rows, :, hh, :], src).then_inc(s_kdiag[u.par], 16)

            def spread_v(u):
                after(sp, v_copied, u)
                for b in range(2):
                    r = 1 - b
                    sp.dma_start(vdiag[u.par][HALF * r:HALF * r + TOK, b, :, HD * r:HD * r + HD],
                                 v[u.par][HALF * b:HALF * b + TOK, :, r, :]).then_inc(s_vdiag[u.par], 16)

            def store(u):
                after(sp, res_ready, u)
                for b in range(2):
                    dst = bass.AP(tensor=out.tensor, offset=(2 * u.n + b) * TOK * HID, ap=[[HID, TOK], [1, HID]])
                    sp.dma_start(dst, res[u.par][HALF * b:HALF * b + TOK, :]).then_inc(s_stored[u.par], 16)

            def load(weights):
                for landed, dst, src in weights:
                    sp.dma_start(dst, src).then_inc(landed, 16)

            load(token_loads)
            sp.wait_ge(s_zeroed, 1)

            def step(t):
                if (t - 3).exists():
                    store(t - 3)
                if (t + 2).exists():
                    if t.static and t.n == -2:
                        sp.wait_ge(s_kdiag_zeroed, 1)
                        sp.wait_ge(s_zeroed, 4)
                    spread_k(t + 2)
                if (t + 1).exists():
                    if t.static and t.n == -1:
                        sp.wait_ge(s_zeroed, 3)
                    spread_v(t + 1)
                if (t + 6).exists():
                    load_blocks(t + 6)
                if t.static and t.n == FIRST_STEP + 1:
                    load(other_loads)

            steps(sp, step)
            for j in range(2):
                sp.wait_ge(s_stored[j], PAIRS // 2 * 2 * 16)

        @block.gpsimd
        def _(pool):
            for t_ in blk:
                last = nc.gpsimd.memset(t_[:], 0.0)
            last.then_inc(s_zeroed, 1)
            nc.gpsimd.memset(half_exp[:], -0.5)
            nc.gpsimd.memset(eps[:], EPS)
            for t_ in blkT + blkT_low:
                last = nc.gpsimd.memset(t_[:].bitcast(F32), 0.0)
            last.then_inc(s_zeroed, 1)
            for t_ in vdiag + prob + [carry]:
                last = nc.gpsimd.memset(t_[:], 0.0)
            last.then_inc(s_zeroed, 1)
            nc.gpsimd.memset(kdiag[1][:], 0.0).then_inc(s_zeroed, 1)
            pool.wait_ge(s_zeroed, 2)

            def inverse_deviation(l, u):
                after(pool, mv_ready[l], u)
                nc.gpsimd.tensor_tensor(veps[l][u.par][:], mv[l][u.par][:, 1:2], eps[:], ALU.add).then_inc(veps_ready[l], 1)
                after(pool, veps_ready[l], u)
                nc.gpsimd.tensor_tensor(rstd[l][u.par][:], veps[l][u.par][:], half_exp[:], ALU.pow).then_inc(rstd_ready[l], 1)

            def attention_residual(u):
                if u.static and u.n == 0:
                    pool.wait_ge(s_outb, 1)
                after(pool, h_ready, u)
                nc.gpsimd.tensor_tensor(resid[:, bass.ds(u.n * HID, HID)], h[u.par][:], outb[:], ALU.add).then_inc(resid_ready, 1)

            def split_xn(u):
                after(pool, xnT_high_ready, u)
                after(pool, v_done, u - 2)
                nc.gpsimd.tensor_tensor(xnT_low[u.par][:], xnT[u.par][:], xnT_high[u.par][:].bitcast(F32), ALU.subtract).then_inc(xnT_low_ready, 1)

            def split_value_weights():
                pool.wait_ge(s_w_qkv, 2 * 16)
                wv = wqkv[:, :, 2 * HID:]
                nc.gpsimd.tensor_copy(wv_high[:], wv).then_inc(s_wv_split, 1)
                pool.wait_ge(s_wv_split, 1)
                nc.gpsimd.tensor_tensor(wv_low[:], wv, wv_high[:].bitcast(F32), ALU.subtract).then_inc(s_wv_split, 1)

            def expert_bias(u):
                after(pool, y_raw_ready, u)
                after(pool, res_ready, u - 2)
                nc.gpsimd.tensor_tensor(y[u.par][:], y_raw[u.par][:, 0:HID], expb[:], ALU.add).then_inc(y_ready, 1)

            def step(t):
                if (t - 2).exists():
                    expert_bias(t - 2)
                if (t + 2).exists():
                    split_xn(t + 2)
                if (t - 1).exists():
                    inverse_deviation(1, t - 1)
                if (t + 3).exists():
                    inverse_deviation(0, t + 3)
                if (t + 2).exists():
                    attention_residual(t + 2)
                if t.static and t.n == -3:
                    split_value_weights()

            steps(pool, step)

        @block.scalar
        def _(act):
            act.wait_ge(s_zeroed, 2)
            nc.scalar.activation(eps_exp[:], eps[:], ACT.Exp)

            def transposed_xn2(u):
                after(act, xn2T_done, u)
                after(act, ffn_done, u - 2)
                nc.scalar.copy(xn2T[u.par][:], ps_t[:, 0:HID]).then_inc(xn2T_ready, 1)

            def exponentials(u):
                after(act, pT_done, u - 2, KC)
                for g in range(KC):
                    act.wait_ge(shifted_ready, u.n * KC + g + 1)
                    part = slice(g * HG, (g + 1) * HG)
                    nc.scalar.activation(prob[u.par][:, part, 0:TOK], shifted[u.par][:, part, :], ACT.Exp).then_inc(prob_ready, 1)

            def values(u):
                after(act, v_done, u)
                after(act, v_ready, u - 2, 2)
                after_dma(act, s_vdiag, u - 2, 2)
                nc.scalar.copy(v[u.par][:].rearrange("k p r d -> k (p r d)"), ps_t[:, 0:HID]).then_inc(v_copied, 1)

            def diagonal_values(u):
                after(act, v_copied, u)
                after(act, pv_done, u - 2)
                for b in range(2):
                    rows = slice(HALF * b, HALF * b + HALF)
                    nc.scalar.copy(vdiag[u.par][rows, b, :, HD * b:HD * b + HD], v[u.par][rows, :, b, :]).then_inc(v_ready, 1)

            def transposed_att(u):
                after(act, attT_done, u)
                after(act, out_done, u - 2)
                nc.scalar.copy(attT[u.par][:], ps_o[:, 0:HID]).then_inc(attT_ready, 1)

            def evacuate_qk(u, chunks, ready):
                for m in chunks:
                    nc.scalar.activation(qk[u.par][:, m, :], ps_qk[:, m, :], ACT.Identity, bias=qkb[:, m:m + 1]).then_inc(ready, 1)

            def keys(u):
                after(act, qk_done, u)
                after_dma(act, s_kdiag, u - 2, HG)
                evacuate_qk(u, range(KC, 2 * KC), k_ready)

            def queries(u):
                after(act, score_done, u - 2)
                evacuate_qk(u, range(KC), q_ready)

            def expert(u):
                after(act, ffn_done, u)
                after(act, y_ready, u - 2)
                after(act, glog_ready, u - 2)
                nc.scalar.copy(y_raw[u.par][:], ps_p[:, 0:HID + EXPERTS]).then_inc(y_raw_ready, 1)

            def gate_sum(u):
                after(act, glog_ready, u)
                nc.scalar.activation(gexp[u.par][:], glog[u.par][:], ACT.Exp, accum_out=gsum[u.par][:]).then_inc(gsum_ready, 1)

            def transposed_blocks(u):
                after(act, blkT_done, u)
                after(act, tok_done, u - 2)
                nc.scalar.copy(blkT[u.par][:, 0:P], ps_t[:, 0:P]).then_inc(blkT_ready, 1)

            def transposed_probs(u):
                after(act, pv_done, u - 2)
                for g in range(KC):
                    if u.exists():
                        act.wait_ge(pT_done, u.n * KC + g + 1)
                    part = slice(g * HP // KC, (g + 1) * HP // KC)
                    nc.scalar.copy(probT[u.par][:, part, :], ps_pT[:, part, :]).then_inc(pT_ready, 1)

            def transposed_xn(u):
                after(act, xnT_done, u)
                after(act, qk_done, u - 2)
                after(act, xnT_low_ready, u - 2)
                nc.scalar.copy(xnT[u.par][:], ps_t[:, 0:HID]).then_inc(xnT_ready, 1)
                after(act, v_done, u - 2)
                nc.scalar.copy(xnT_high[u.par][:], ps_t[:, 0:HID]).then_inc(xnT_high_ready, 1)

            def step(t):
                if t.static and t.n == -1:
                    act.wait_ge(s_zeroed, 3)
                if (t + 2).exists():
                    transposed_xn(t + 2)
                if (t - 2).exists():
                    expert(t - 2)
                if (t - 1).exists():
                    transposed_att(t - 1)
                if t.exists():
                    exponentials(t)
                early = t.static and t.n == -2
                if early:
                    transposed_blocks(t + 4)
                if (t + 2).exists():
                    keys(t + 2)
                if (t + 1).exists():
                    values(t + 1)
                if t.exists():
                    transposed_probs(t)
                if (t + 4).exists() and not early:
                    transposed_blocks(t + 4)
                if (t + 2).exists():
                    queries(t + 2)
                if (t - 2).exists():
                    gate_sum(t - 2)
                if (t + 1).exists():
                    diagonal_values(t + 1)
                if (t - 1).exists():
                    transposed_xn2(t - 1)

            steps(act, step)

        @block.vector
        def _(dve):
            def window_weights():
                dve.wait_ge(s_w_tok, 4 * 16)
                for c in range(KC):
                    nc.vector.tensor_scalar(wtok[:, c, :], wtok[:, c, :], win[:, c:c + 1], None, ALU.mult).then_inc(s_wtok, 1)

            def split(landed, count, w, high, low, parts_ready):
                dve.wait_ge(landed, count)
                nc.vector.tensor_copy(high[:], w[:]).then_inc(parts_ready, 1)
                dve.wait_ge(parts_ready, 1)
                nc.vector.tensor_tensor(low[:], w[:], high[:].bitcast(F32), ALU.subtract).then_inc(parts_ready, 1)

            def low_part(u, high_ready, transposed, high, low, low_ready):
                after(dve, high_ready, u)
                nc.vector.tensor_tensor(low, transposed, high.bitcast(F32), ALU.subtract).then_inc(low_ready, 1)

            def low_blocks(u):
                low_part(u, blkT_ready, ps_t[:, 0:P], blkT[u.par][:, 0:P], blkT_low[u.par][:, 0:P], blkT_low_ready)

            def low_att(u):
                low_part(u, attT_ready, ps_o[:, 0:HID], attT[u.par][:].rearrange("f c q -> f (c q)"),
                         attT_low[u.par][:].rearrange("f c q -> f (c q)"), attT_low_ready)

            def low_xn2(u):
                low_part(u, xn2T_ready, ps_t[:, 0:HID], xn2T[u.par][:].rearrange("f c q -> f (c q)"),
                         xn2T_low[u.par][:].rearrange("f c q -> f (c q)"), xn2T_low_ready)

            def value_bias():
                dve.wait_ge(s_w_qkv, 2 * 16)
                dve.wait_ge(s_zeroed, 3)
                for c in range(KC):
                    nc.vector.tensor_scalar(vb_wide[:, c, :], vb[:, c:c + 1].to_broadcast([P, P]), 1.0 / HID ** 0.5, None, ALU.mult).then_inc(s_vb_wide, 1)
                for j in range(2):
                    for r in range(2):
                        last = nc.vector.memset(vdiag[j][HALF * r:HALF * r + TOK, :, :, 2 * HD + r], HID ** 0.5)
                last.then_inc(s_vb_wide, 1)

            def output_bias():
                dve.wait_ge(s_w_out, 2 * 16)
                dve.wait_ge(s_vb_mm, 1)
                nc.vector.tensor_tensor(outb[:], ps_p[:, 0:HID], outb[:], ALU.add).then_inc(s_outb, 1)

            def token_order():
                dve.wait_ge(s_w_ffn, 4 * 16)
                nc.vector.tensor_copy(order[:], order_f[:, 0:2 * P]).then_inc(s_order, 1)

            def aggregate(l, u):
                nc.vector.bn_aggr(mv[l][u.par][:], stat[l][u.par][:]).then_inc(mv_ready[l], 1)

            def residual(u):
                after(dve, res_ready, u - 2)
                after(dve, out_done, u)
                after(dve, resid_ready, u)
                nc.vector.tensor_tensor(h2[u.par][:], ps_p[:, 0:HID], resid[:, bass.ds(u.n * HID, HID)], ALU.add).then_inc(h2_ready, 1)
                after(dve, h2_ready, u)
                nc.vector.bn_stats(stat[1][u.par][:], h2[u.par][:]).then_inc(stat_ready[1], 1)

            def normalize2(u):
                after(dve, rstd_ready[1], u)
                after(dve, xn2T_done, u - 2)
                nc.vector.tensor_scalar(xn2[u.par][:], h2[u.par][:], mv[1][u.par][:, 0:1], rstd[1][u.par][:], ALU.subtract, ALU.mult).then_inc(xn2_ready, 1)

            def gate_value(u):
                after(dve, gsum_ready, u)
                nc.vector.reciprocal(gate[u.par][:], gsum[u.par][:]).then_inc(gate_ready, 1)

            def queue_places(u):
                j = u.par
                after(dve, count_done, u)
                after(dve, carry_ready, u - 1)
                nc.vector.tensor_tensor(place[j][:], ps_qk[:, 0, 0:EXPERTS], carry[:], ALU.add).then_inc(place_ready, 1)
                nc.vector.tensor_tensor(carry[:], ps_qk[:, 0, EXPERTS:2 * EXPERTS], carry[:], ALU.add).then_inc(carry_ready, 1)

            def gate_weight(u):
                j = u.par
                after(dve, place_ready, u)
                nc.vector.scalar_tensor_tensor(keep8[j][:], place[j][:], float(CAPACITY), mask[j][:], ALU.is_le, ALU.mult,
                                               accum_out=kept[j][:]).then_inc(kept_ready, 1)
                after(dve, kept_ready, u)
                after(dve, gate_ready, u)
                nc.vector.tensor_tensor(weight[j][:], kept[j][:], gate[j][:], ALU.mult).then_inc(weight_ready, 1)

            def result(u):
                after(dve, weight_ready, u)
                after(dve, y_ready, u)
                after_dma(dve, s_stored, u - 2, 2)
                nc.vector.scalar_tensor_tensor(res[u.par][:], y[u.par][:], weight[u.par][:], h2[u.par][:], ALU.mult, ALU.add).then_inc(res_ready, 1)

            def maximum(u):
                after(dve, score_done, u)
                nc.vector.tensor_reduce(top[u.par][:].rearrange("q (g h) -> q g h", g=KC),
                                        ps_s[:, :, 0:HG * TOK].rearrange("q g (h k) -> q g h k", h=HG), AX.X, ALU.max).then_inc(top_ready, 1)
                after(dve, top_ready, u)
                after(dve, prob_ready, u - 2, KC)

            def shift(u, g):
                part = slice(g * HG, (g + 1) * HG)
                nc.vector.tensor_tensor(shifted[u.par][:, part, :], ps_s[:, g, 0:HG * TOK].rearrange("q (h k) -> q h k", h=HG),
                                        top[u.par][:, part].unsqueeze(2).to_broadcast([P, HG, TOK]), ALU.subtract).then_inc(shifted_ready, 1)

            def logits(u):
                j = u.par
                after(dve, y_raw_ready, u)
                nc.vector.tensor_reduce(gtop[j][:], y_raw[j][:, HID:], AX.X, ALU.max).then_inc(gtop_ready, 1)
                after(dve, gtop_ready, u)
                nc.vector.tensor_scalar(glog[j][:], y_raw[j][:, HID:], gtop[j][:], None, ALU.subtract).then_inc(glog_ready, 1)

            def best_expert(u):
                j = u.par
                after(dve, glog_ready, u)
                nc.vector.scalar_tensor_tensor(ghit[j][:], glog[j][:], 0.0, rank, ALU.is_ge, ALU.mult).then_inc(ghit_ready, 1)
                after(dve, ghit_ready, u)
                nc.vector.tensor_reduce(gbest[j][:], ghit[j][:], AX.X, ALU.max).then_inc(gbest_ready, 1)
                after(dve, gbest_ready, u)
                nc.vector.tensor_scalar(mask[j][:], rank, gbest[j][:], None, ALU.is_equal).then_inc(mask_ready, 1)

            def tokens(u):
                after(dve, tok_done, u)
                after(dve, resid_ready, u - 2)
                nc.vector.tensor_tensor(h[u.par][:], ps_p[:, 0:HID], tokb[:], ALU.add).then_inc(h_ready, 1)

            def token_statistics(u):
                after(dve, h_ready, u)
                nc.vector.bn_stats(stat[0][u.par][:], h[u.par][:]).then_inc(stat_ready[0], 1)

            def normalize(u):
                after(dve, rstd_ready[0], u)
                after(dve, xnT_done, u - 2)
                nc.vector.tensor_scalar(xn[u.par][:], h[u.par][:], mv[0][u.par][:, 0:1], rstd[0][u.par][:], ALU.subtract, ALU.mult).then_inc(xn_ready, 1)

            def inverse_sums(u):
                after(dve, pv_done, u)
                nc.vector.reciprocal(rsum[u.par][:], ps_pv[:, :, 2 * HD:]).then_inc(rsum_ready, 1)

            def attention_out(u):
                after(dve, rsum_ready, u)
                after(dve, attT_done, u - 2)
                nc.vector.tensor_tensor(att[u.par][:].rearrange("q (p r d) -> q p r d", p=HP, r=2),
                                        ps_pv[:, :, 0:2 * HD].rearrange("q p (r d) -> q p r d", r=2),
                                        rsum[u.par][:].unsqueeze(3).to_broadcast([P, HP, 2, HD]), ALU.mult).then_inc(att_ready, 1)

            def step(t):
                if (t + 2).exists():
                    normalize(t + 2)
                if (t - 1).exists():
                    inverse_sums(t - 1)
                if (t - 3).exists():
                    result(t - 3)
                if (t - 1).exists():
                    attention_out(t - 1)
                if t.exists():
                    maximum(t)
                if (t - 1).exists():
                    low_att(t - 1)
                if t.exists():
                    shift(t, 0)
                    shift(t, 1)
                if (t - 2).exists():
                    logits(t - 2)
                if (t - 1).exists():
                    residual(t - 1)
                    after(dve, stat_ready[1], t - 1)
                if (t - 2).exists():
                    best_expert(t - 2)
                if (t - 1).exists():
                    aggregate(1, t - 1)
                filling = t.static and t.n < 0
                if (t + 4).exists() and not filling:
                    low_blocks(t + 4)
                if (t - 1).exists():
                    normalize2(t - 1)
                if (t + 3).exists():
                    tokens(t + 3)
                if t.static and t.n == -2:
                    output_bias()
                if filling and (t + 3).exists():
                    token_statistics(t + 3)
                    after(dve, stat_ready[0], t + 3)
                    aggregate(0, t + 3)
                if (t + 4).exists() and filling:
                    low_blocks(t + 4)
                if (t + 3).exists() and not filling:
                    token_statistics(t + 3)
                    after(dve, stat_ready[0], t + 3)
                if (t - 2).exists():
                    gate_value(t - 2)
                if (t + 3).exists() and not filling:
                    aggregate(0, t + 3)
                if (t - 2).exists():
                    queue_places(t - 2)
                    gate_weight(t - 2)
                if (t - 1).exists():
                    low_xn2(t - 1)
                if t.static and t.n == -3:
                    value_bias()
                if t.static and t.n == -1:
                    split(s_w_out, 2 * 16, wout, wout_high, wout_low, s_wout_split)
                if t.static and t.n == 0:
                    split(s_w_ffn, 4 * 16, wffn, wffn_high, wffn_low, s_wffn_split)
                    token_order()

            nc.vector.memset(warm[:], 0.0).then_inc(s_warm, 1)
            nc.vector.memset(kdiag[0][:], 0.0).then_inc(s_kdiag_zeroed, 1)
            window_weights()
            split(s_wtok, KC, wtok, wtok_high, wtok_low, s_wtok_split)
            steps(dve, step)

        @block.tensor
        def _(pe):
            pe.wait_ge(s_warm, 1)
            for _ in range(WARM_UP):
                nc.tensor.matmul(ps_t[:], warm[:, 0:P], warm[:], start=True, stop=True)
            pe.wait_ge(s_w_tok, 4 * 16)

            def product(u, psum, data, data_low, data_low_ready, high, low, parts_ready, done, cols, first_low=2):
                terms = [(data, high), (data, low), (data_low, high)]
                for k, (a, w) in enumerate(terms):
                    if u.static:
                        pe.wait_ge(parts_ready, 1 + k % 2)
                    if k == first_low:
                        after(pe, data_low_ready, u)
                    for c in range(KC):
                        last = nc.tensor.matmul(psum, cols(a[u.par], c), w[:, c, :], start=(k == 0 and c == 0), stop=(k == 2 and c == KC - 1))
                last.then_inc(done, 1)

            def output_bias():
                pe.wait_ge(s_w_out, 2 * 16)
                pe.wait_ge(s_vb_wide, KC + 1)
                pe.wait_ge(h_ready, 2)
                for c in range(KC):
                    last = nc.tensor.matmul(ps_p[:, 0:HID], vb_wide[:, c, :], wout[:, c, :], start=(c == 0), stop=(c == KC - 1))
                last.then_inc(s_vb_mm, 1)

            def transpose_blocks(u):
                after_dma(pe, s_blocks, u, 2)
                after_latest(pe, (v_copied, u - 3, 1), (xnT_high_ready, u - 2, 1), (blkT_low_ready, u - 1, 1))
                nc.tensor.transpose(ps_t[:, 0:P], blk[u.par][:], ident[:]).then_inc(blkT_done, 1)

            def tokens(u):
                after(pe, blkT_ready, u)
                if u.static and u.n == 2:
                    pe.wait_ge(s_outb, 1)
                after_latest(pe, (h2_ready, u - 4, 1), (h_ready, u - 1, 1))
                product(u, ps_p[:, 0:HID], blkT, blkT_low, blkT_low_ready, wtok_high, wtok_low, s_wtok_split, tok_done,
                        lambda a, c: a[:, 2 * c:2 * c + P])

            def transpose_xn(u):
                after(pe, xn_ready, u)
                after_latest(pe, (xn2T_low_ready, u - 4, 1), (blkT_low_ready, u + 1, 1))
                for c in range(KC):
                    last = nc.tensor.transpose(ps_t[:, P * c:P * c + P], xn[u.par][:, P * c:P * c + P], ident[:])
                last.then_inc(xnT_done, 1)

            def queries_keys(u):
                after(pe, xnT_ready, u)
                after_latest(pe, (carry_ready, u - 5, 1), (q_ready, u - 1, KC))
                for m in range(2 * KC):
                    for c in range(KC):
                        last = nc.tensor.matmul(ps_qk[:, m, :], wqkv[:, c, P * m:P * m + P], xnT[u.par][:, c, :], start=(c == 0), stop=(c == KC - 1))
                last.then_inc(qk_done, 1)

            def values(u):
                after_latest(pe, (xnT_high_ready, u + 1, 1), (xn2T_low_ready, u - 3, 1))
                product(u, ps_t[:, 0:HID], xnT_high, xnT_low, xnT_low_ready, wv_high, wv_low, s_wv_split, v_done,
                        lambda a, c: a[:, c, :], first_low=0)

            def scores(u):
                after_dma(pe, s_kdiag, u, HG)
                after(pe, q_ready, u, KC)
                after(pe, shifted_ready, u - 1, KC)
                for g in range(KC):
                    for b in range(2):
                        last = nc.tensor.matmul(ps_s[HALF * b:HALF * b + HALF, g, 0:HG * TOK],
                                                qk[u.par][:, g, HALF * b:HALF * b + HALF],
                                                kdiag[u.par][:, 2 * g + b, :, :].rearrange("p h k -> p (h k)"), start=True, stop=True)
                last.then_inc(score_done, 1)

            def transpose_probs(u):
                after(pe, pT_ready, u - 1, KC)
                for p in range(HP):
                    if p % (HP // KC) == 0:
                        pe.wait_ge(prob_ready, u.n * KC + p // (HP // KC) + 1)
                    last = nc.tensor.transpose(ps_pT[:, p, :], prob[u.par][:, 2 * p:2 * p + 2, :].rearrange("q h k -> q (h k)"), ident[:])
                    if p % (HP // KC) == HP // KC - 1:
                        last.then_inc(pT_done, 1)

            def weighted_values(u):
                after(pe, v_ready, u, 2)
                after_dma(pe, s_vdiag, u, 2)
                after(pe, attT_low_ready, u - 1)
                for g in range(KC):
                    pe.wait_ge(pT_ready, u.n * KC + g + 1)
                    for p in range(g * HP // KC, (g + 1) * HP // KC):
                        for b in range(2):
                            last = nc.tensor.matmul(ps_pv[HALF * b:HALF * b + HALF, p, :], probT[u.par][:, p, HALF * b:HALF * b + HALF],
                                                    vdiag[u.par][:, b, p, :], start=True, stop=True)
                last.then_inc(pv_done, 1)

            def transpose_att(u):
                after(pe, att_ready, u)
                for c in range(KC):
                    last = nc.tensor.transpose(ps_o[:, P * c:P * c + P], att[u.par][:, P * c:P * c + P], ident[:])
                last.then_inc(attT_done, 1)

            def project(u):
                after(pe, attT_ready, u)
                after_latest(pe, (y_raw_ready, u - 1, 1), (h_ready, u + 3, 1))
                product(u, ps_p[:, 0:HID], attT, attT_low, attT_low_ready, wout_high, wout_low, s_wout_split, out_done,
                        lambda a, c: a[:, c, :])

            def transpose_xn2(u):
                after(pe, xn2_ready, u)
                after_latest(pe, (blkT_low_ready, u + 5, 1), (v_copied, u + 2, 1), (xn2T_low_ready, u - 1, 1))
                for c in range(KC):
                    last = nc.tensor.transpose(ps_t[:, P * c:P * c + P], xn2[u.par][:, P * c:P * c + P], ident[:])
                last.then_inc(xn2T_done, 1)

            def expert(u):
                after(pe, xn2T_ready, u)
                after_latest(pe, (h_ready, u + 4, 1), (h2_ready, u, 1))
                product(u, ps_p[:, 0:HID + EXPERTS], xn2T, xn2T_low, xn2T_low_ready, wffn_high, wffn_low, s_wffn_split, ffn_done,
                        lambda a, c: a[:, c, :])

            def counts(u):
                if u.static and u.n == 0:
                    pe.wait_ge(s_order, 1)
                after(pe, mask_ready, u)
                after_latest(pe, (q_ready, u + 4, KC), (carry_ready, u - 1, 1))
                for c in range(2):
                    last = nc.tensor.matmul(ps_qk[:, 0, EXPERTS * c:EXPERTS * (c + 1)], order[:, P * c:P * c + P], mask[u.par][:], start=True, stop=True)
                last.then_inc(count_done, 1)

            def step(t):
                if t.static and t.n == -2:
                    pe.wait_ge(s_w_qkv, 2 * 16)
                if t.exists():
                    scores(t)
                if (t + 2).exists():
                    transpose_xn(t + 2)
                if t.static and t.n == -2:
                    output_bias()
                    transpose_blocks(t + 4)
                if (t - 2).exists():
                    expert(t - 2)
                if (t - 1).exists():
                    transpose_att(t - 1)
                if (t + 2).exists():
                    queries_keys(t + 2)
                if (t - 1).exists():
                    project(t - 1)
                if (t + 1).exists():
                    values(t + 1)
                if t.exists():
                    transpose_probs(t)
                if (t + 3).exists() and not (t.static and t.n == -2):
                    tokens(t + 3)
                if (t + 4).exists() and not (t.static and t.n == -2):
                    transpose_blocks(t + 4)
                if t.exists():
                    weighted_values(t)
                if (t - 2).exists():
                    counts(t - 2)
                if (t - 1).exists():
                    transpose_xn2(t - 1)
                if t.static and t.n == -3:
                    tokens(t + 4)

            steps(pe, step)


_INS = ["x", "L0_tok_W", "L0_tok_b", "L0_attn_W_qkv", "L0_attn_b_qkv", "L0_attn_W_out", "L0_attn_b_out",
        "L0_ffn_w_gate", "L0_ffn_w_expert", "L0_ffn_b_expert"]


def kernel(**inputs):
    import numpy as np
    import concourse.bacc as bacc
    from concourse.bass_utils import run_bass_kernel_spmd

    window = np.hanning(FRAME).astype(np.float32).reshape(KC, P).T
    ident = np.eye(P, dtype=np.float32)
    real = (np.arange(P) % HALF < TOK)[:, None]
    upto = np.arange(P)[:, None] <= np.arange(P)[None, :]
    rank = np.broadcast_to(EXPERTS - np.arange(EXPERTS), (P, EXPERTS))
    order = np.concatenate([upto & real, np.broadcast_to(real, (P, P)), rank], 1).astype(np.float32)

    inputs = dict(inputs, L0_attn_b_qkv=np.asarray(inputs["L0_attn_b_qkv"]).reshape(3 * KC, P).T)

    nc = bacc.Bacc("TRN2", target_bir_lowering=False, num_devices=1)
    arrays, args = {}, []
    consts = {"window": window, "ident": ident, "order": order}
    for name in _INS + list(consts):
        a = np.ascontiguousarray(consts[name] if name in consts else inputs[name])
        arrays[f"in_{name}"] = a
        args.append(nc.dram_tensor(f"in_{name}", a.shape, mybir.dt.from_np(a.dtype), kind="ExternalInput").ap())
    out = nc.dram_tensor("out", (BATCH, TOK, HID), F32, kind="ExternalOutput").ap()
    audio_tower(nc, *args, out)
    r = run_bass_kernel_spmd(nc, [arrays], core_ids=[0])
    return r.results[0]["out"]
```
